# Optimizing a Trainium2 kernel written in Bass

```python
import numpy as np
import jax
import jax.numpy as jnp

def _softmax(x, axis=-1):
    return jax.nn.softmax(x, axis=axis)

def _gelu(x):
    return jax.nn.gelu(x, approximate=True)

def _silu(x):
    return jax.nn.silu(x)

def _sigmoid(x):
    return jax.nn.sigmoid(x)

def _layernorm(x, axis=-1, eps=1e-05):
    m = jnp.mean(x, axis=axis, keepdims=True)
    v = jnp.var(x, axis=axis, keepdims=True)
    return (x - m) / jnp.sqrt(v + eps)

def _scatter_add(tgt, idx, src, axis=0):
    return tgt.at[idx].add(src)

def _segment_sum(src, seg, n):
    return jax.ops.segment_sum(src, seg, n)
kernel_name = 'mk_gnn_resnorm_d2_gnn_r32_1b0e1d'

def setup_inputs(seed: int=0):
    np.random.seed(seed)
    _w = jnp.asarray

    def _rec_inputs():
        import jax
        import jax.numpy as jnp
        _gk = jax.random.key(seed)
        x = -0.0003713 + 1 * jax.random.normal(jax.random.fold_in(_gk, 1), (3125, 128), jnp.float32)
        _s = jax.random.randint(jax.random.fold_in(_gk, 2), (25000,), 0, 3125, jnp.int32)
        _d = jax.random.randint(jax.random.fold_in(_gk, 3), (25000,), 0, 3125, jnp.int32)
        _loop = jnp.arange(3125, dtype=jnp.int32)
        src = jnp.concatenate([_s, _d, _loop])
        dst = jnp.concatenate([_d, _s, _loop])
        _o = jnp.argsort(dst, stable=True)
        src = src[_o]
        dst = dst[_o]
        edge_type_3 = jax.random.randint(jax.random.fold_in(_gk, 13), (53125,), 0, 3, jnp.int32)
        edge_weight = jax.random.uniform(jax.random.fold_in(_gk, 14), (53125,), jnp.float32, 0.0, 0.999999)
        return (x, src, dst, edge_type_3, edge_weight)
    x, src, dst, edge_type_3, edge_weight = _rec_inputs()

    def _L0_gnn_setup():
        import jax, jax.numpy as jnp
        import numpy as np
        N_NODES = 3125
        N_EDGES = 50000
        IN_FEATS = 128
        HIDDEN = 150
        NUM_OUT = 128

        def _mean_agg(h, src, dst, deg_inv):
            summed = jax.ops.segment_sum(h[src], dst, num_segments=N_NODES)
            return summed * deg_inv[:, None]

        def _sage_conv(h, src, dst, deg_inv, W_self, W_neigh, b):
            h_neigh = _mean_agg(h, src, dst, deg_inv)
            return h @ W_self + h_neigh @ W_neigh + b
        key = jax.random.key(seed)
        ks = jax.random.split(key, 9)
        x = jax.random.normal(ks[0], (N_NODES, IN_FEATS), dtype=jnp.float32)
        src = jax.random.randint(ks[1], (N_EDGES,), 0, N_NODES, dtype=jnp.int32)
        dst = jax.random.randint(ks[2], (N_EDGES,), 0, N_NODES, dtype=jnp.int32)

        def lin(k, fan_in, fan_out):
            bound = 1.0 / np.sqrt(fan_in)
            return jax.random.uniform(k, (fan_in, fan_out), jnp.float32, -bound, bound)
        W_self1 = lin(ks[3], IN_FEATS, HIDDEN)
        W_neigh1 = lin(ks[4], IN_FEATS, HIDDEN)
        b1 = jnp.zeros((HIDDEN,), jnp.float32)
        W_self2 = lin(ks[5], HIDDEN, NUM_OUT)
        W_neigh2 = lin(ks[6], HIDDEN, NUM_OUT)
        b2 = jnp.zeros((NUM_OUT,), jnp.float32)
        return {'x': x, 'src': src, 'dst': dst, 'W_self1': W_self1, 'W_neigh1': W_neigh1, 'b1': b1, 'W_self2': W_self2, 'W_neigh2': W_neigh2, 'b2': b2}
    _L0_gnn_all = _L0_gnn_setup()
    _L0_gnn_in = {k: v for k, v in _L0_gnn_all.items() if k in ('W_self1', 'W_neigh1', 'b1', 'W_self2', 'W_neigh2', 'b2')}
    del _L0_gnn_all

    def _L1_gnn_setup():
        import jax, jax.numpy as jnp
        import numpy as np
        N_NODES = 50000
        N_EDGES = 18750
        EMB_DIM = 128
        N_REL = 3
        BN_EPS = 1e-05
        key = jax.random.key(seed)
        k1, k2, k3, k4, k5 = jax.random.split(key, 5)
        node_features = jax.random.normal(k1, (N_NODES, EMB_DIM), dtype=jnp.float32)
        edge_index = jax.random.randint(k2, (2, N_EDGES), 0, N_NODES, dtype=jnp.int64)
        edge_type = jax.random.randint(k3, (N_EDGES,), 0, N_REL, dtype=jnp.int64)
        edge_weight = jax.random.uniform(k4, (N_EDGES,), dtype=jnp.float32)
        W = jax.random.normal(k5, (N_REL, EMB_DIM, EMB_DIM), dtype=jnp.float32) / np.sqrt(EMB_DIM)
        gamma = jnp.ones((EMB_DIM,), dtype=jnp.float32)
        beta = jnp.zeros((EMB_DIM,), dtype=jnp.float32)
        running_mean = jnp.zeros((EMB_DIM,), dtype=jnp.float32)
        running_var = jnp.ones((EMB_DIM,), dtype=jnp.float32)
        return {'node_features': node_features, 'edge_index': edge_index, 'edge_type': edge_type, 'edge_weight': edge_weight, 'W': W, 'gamma': gamma, 'beta': beta, 'running_mean': running_mean, 'running_var': running_var}
    _L1_gnn_all = _L1_gnn_setup()
    _L1_gnn_in = {k: v for k, v in _L1_gnn_all.items() if k in ('W', 'gamma', 'beta', 'running_mean', 'running_var')}
    del _L1_gnn_all
    return {'x': x, 'src': src, 'dst': dst, 'edge_type_3': edge_type_3, 'edge_weight': edge_weight, 'L0_gnn_W_self1': _L0_gnn_in['W_self1'], 'L0_gnn_W_neigh1': _L0_gnn_in['W_neigh1'], 'L0_gnn_b1': _L0_gnn_in['b1'], 'L0_gnn_W_self2': _L0_gnn_in['W_self2'], 'L0_gnn_W_neigh2': _L0_gnn_in['W_neigh2'], 'L0_gnn_b2': _L0_gnn_in['b2'], 'L1_gnn_W': _L1_gnn_in['W'], 'L1_gnn_gamma': _L1_gnn_in['gamma'], 'L1_gnn_beta': _L1_gnn_in['beta'], 'L1_gnn_running_mean': _L1_gnn_in['running_mean'], 'L1_gnn_running_var': _L1_gnn_in['running_var']}

def reference(x, src, dst, edge_type_3, edge_weight, L0_gnn_W_self1, L0_gnn_W_neigh1, L0_gnn_b1, L0_gnn_W_self2, L0_gnn_W_neigh2, L0_gnn_b2, L1_gnn_W, L1_gnn_gamma, L1_gnn_beta, L1_gnn_running_mean, L1_gnn_running_var):
    import jax
    import jax.numpy as jnp

    def _L0_gnn_ref(x, src, dst, W_self1, W_neigh1, b1, W_self2, W_neigh2, b2):
        import jax, jax.numpy as jnp
        import numpy as np
        N_NODES = 3125
        N_EDGES = 50000
        IN_FEATS = 128
        HIDDEN = 150
        NUM_OUT = 128

        def _mean_agg(h, src, dst, deg_inv):
            summed = jax.ops.segment_sum(h[src], dst, num_segments=N_NODES)
            return summed * deg_inv[:, None]

        def _sage_conv(h, src, dst, deg_inv, W_self, W_neigh, b):
            h_neigh = _mean_agg(h, src, dst, deg_inv)
            return h @ W_self + h_neigh @ W_neigh + b
        deg = jax.ops.segment_sum(jnp.ones((src.shape[0],), x.dtype), dst, num_segments=N_NODES)
        deg_inv = jnp.where(deg > 0, 1.0 / jnp.maximum(deg, 1.0), 0.0)
        h = _sage_conv(x, src, dst, deg_inv, W_self1, W_neigh1, b1)
        h = jax.nn.relu(h)
        h = _sage_conv(h, src, dst, deg_inv, W_self2, W_neigh2, b2)
        return h

    def _L1_gnn_ref(node_features, edge_index, edge_type, edge_weight, W, gamma, beta, running_mean, running_var):
        import jax, jax.numpy as jnp
        import numpy as np
        N_NODES = 50000
        N_EDGES = 18750
        EMB_DIM = 128
        N_REL = 3
        BN_EPS = 1e-05
        src, dst = (edge_index[0], edge_index[1])
        src_feats = node_features[src]
        scale_r1 = (edge_weight + 1.0) * 0.5
        msgs = jnp.zeros_like(src_feats)
        for r in range(W.shape[0]):
            t = src_feats @ W[r].T
            if r == 1:
                t = t * scale_r1[:, None]
            mask = (edge_type == r).astype(t.dtype)[:, None]
            msgs = msgs + t * mask
        out = jax.ops.segment_sum(msgs, dst, num_segments=node_features.shape[0])
        out = out + node_features
        out = (out - running_mean) * jax.lax.rsqrt(running_var + BN_EPS) * gamma + beta
        return jax.nn.relu(out)
    edge_index = jnp.stack([src, dst])
    x = _layernorm(x + _L0_gnn_ref(x, src, dst, L0_gnn_W_self1, L0_gnn_W_neigh1, L0_gnn_b1, L0_gnn_W_self2, L0_gnn_W_neigh2, L0_gnn_b2), axis=-1)
    x = _layernorm(x + _L1_gnn_ref(x, edge_index, edge_type_3, edge_weight, L1_gnn_W, L1_gnn_gamma, L1_gnn_beta, L1_gnn_running_mean, L1_gnn_running_var), axis=-1)
    return x

_drawn_inputs = setup_inputs


def setup_inputs(seed=0):
    import zlib

    import numpy as np

    out = dict(_drawn_inputs(seed))
    spreads = {'L0_gnn_b1': (0.0, 0.1),
     'L0_gnn_b2': (0.0, 0.1),
     'L1_gnn_gamma': (1.0, 0.2),
     'L1_gnn_beta': (0.0, 0.308),
     'L1_gnn_running_mean': (0.0, 0.297),
     'L1_gnn_running_var': (1.0, 0.2)}
    factors = {}
    for name, (base, spread) in spreads.items():
        noise = np.random.default_rng([zlib.crc32(name.encode()), seed]).standard_normal(out[name].shape)
        drawn = base * np.exp(spread * noise) if base else spread * noise
        out[name] = jnp.asarray(drawn.astype(out[name].dtype))
    for name, factor in factors.items():
        out[name] = (out[name] * factor).astype(out[name].dtype)
    return out
```

```python
from contextlib import ExitStack

import concourse.bass as bass
from concourse import mybir

F32 = mybir.dt.float32
I32 = mybir.dt.int32
ALU = mybir.AluOpType
ACT = mybir.ActivationFunctionType

P = 125
SLOTS = 5
BANK = 512
ROUND = 12582912.0


def gnn_block(nc, x, src, dst, etype, ew, w_self1, w_neigh1, b1, w_self2, w_neigh2, b2,
              w_rel, gamma, beta, run_mean, run_var, out):
    N, F = x.shape
    E = src.shape[0]
    H = w_self1.shape[1]
    R = w_rel.shape[0]
    TILES, CHUNKS = N // P, E // P
    H2 = H - F
    TRIPS = CHUNKS // SLOTS
    DTRIPS = TILES // SLOTS
    ACC = TILES * F
    BANKS = -(-ACC // BANK)
    LAYERS = 3
    assert N == TILES * P and E == CHUNKS * P and TRIPS * SLOTS == CHUNKS and DTRIPS * SLOTS == TILES

    with ExitStack() as ctx:
        def sb(name, shape, dt=F32):
            return ctx.enter_context(nc.sbuf_tensor(name, shape, dt))

        def sem(name):
            return ctx.enter_context(nc.semaphore(name))

        def sems(name, n=SLOTS):
            return [sem(f"{name}{k}") for k in range(n)]

        g_table = nc.dram_tensor("g_table", (N, F), F32).ap()
        y_table = nc.dram_tensor("y_table", (R * N, F), F32).ap()

        acc = ctx.enter_context(nc.psum_tensor("acc", [128, 8 * BANK], F32))
        DEG = BANKS * BANK

        x_sb = sb("x_sb", [P, TILES, F])
        mean_sb = sb("mean_sb", [P, TILES, F])
        self_sb = sb("self_sb", [P, TILES, F])
        src_i = sb("src_i", [P, CHUNKS], I32)
        dst_i = sb("dst_i", [P, CHUNKS], I32)
        typ_i = sb("typ_i", [P, CHUNKS], I32)
        rel_i = sb("rel_i", [P, CHUNKS], I32)
        dst_f = sb("dst_f", [P, CHUNKS])
        dst_hi = sb("dst_hi", [P, CHUNKS])
        dst_lo = sb("dst_lo", [P, CHUNKS])
        src_f = sb("src_f", [P, CHUNKS])
        typ_f = sb("typ_f", [P, CHUNKS])
        is_r1 = sb("is_r1", [P, CHUNKS])
        w_sb = sb("w_sb", [P, CHUNKS])
        scale = sb("scale", [P, CHUNKS])
        node_iota = sb("node_iota", [P, N])
        ident = sb("ident", [128, 128])
        zeros = sb("zeros", [P, P])
        idx = sb("idx", [P, SLOTS], I32)
        feat = sb("feat", [P, SLOTS, F])
        onehot = sb("onehot", [P, SLOTS, N])
        w1s = sb("w1s", [F, H])
        w1n = sb("w1n", [F, H])
        w2 = sb("w2", [F, 2 * F])
        w2t = sb("w2t", [H2, 2 * F])
        b1a = sb("b1a", [F, 1])
        b1b = sb("b1b", [H2, 1])
        b2r = sb("b2r", [P, F])
        wr = sb("wr", [F, R, F])
        wrT = sb("wrT", [F, R, F])
        bn = sb("bn", [P, 4, F])
        bn_a = sb("bn_a", [P, F])
        bn_b = sb("bn_b", [P, F])
        row_x = sb("row_x", [P, SLOTS, F])
        row_m = sb("row_m", [P, SLOTS, F])
        cols = sb("cols", [F, SLOTS, 2, 128])
        hT = sb("hT", [F, SLOTS, P])
        hTt = sb("hTt", [H2, SLOTS, P])
        g_sb = sb("g_sb", [P, TILES, F])
        y_sb = onehot[:].rearrange("p s n -> p (s n)")[:, 0:TILES * R * F].rearrange("p (t f) -> p t f", t=TILES)
        stats = sb("stats", [P, TILES, 6])
        mv = sb("mv", [P, TILES, 2])
        rstd = sb("rstd", [P, TILES])
        deg = sb("deg", [P, TILES])
        deg_inv = sb("deg_inv", [P, TILES])
        bn_s = sb("bn_s", [P, F])
        lo_hot = sb("lo_hot", [P, SLOTS, P])
        hi_hot = sb("hi_hot", [P, SLOTS, TILES])
        eps = sb("eps", [128, 1])

        loaded = sems("loaded", 5)
        X_IN, EDGES_IN, W_IN, TYPES_IN, BN_IN = loaded
        const_made = sem("const_made")
        ident_made = sem("ident_made")
        dve_step = sem("dve_step")
        idx_ready = sems("idx_ready")
        landed = sems("landed")
        onehot_ready = sems("onehot_ready")
        chunk_done = sems("chunk_done")
        issued = sem("issued")
        deg_ready = sem("deg_ready")
        deg_hot = sems("deg_hot")
        deg_used = sems("deg_used")
        wr_turned = sem("wr_turned")
        wr_kept = sem("wr_kept")
        deg_kept = sem("deg_kept")
        mean_ready = sem("mean_ready")
        rows_ready = sems("rows_ready")
        turned = sems("turned")
        cols_ready = sems("cols_ready")
        h_ready = sems("h_ready")
        relu_done = sems("relu_done")
        g_ready = sems("g_ready")
        g_kept = sems("g_kept")
        g_stored = sems("g_stored")
        x1_ready = sem("x1_ready")
        sqrt_wait = sem("sqrt_wait")
        stats_made = sem("stats_made")
        sqrt_done = sem("sqrt_done")
        rows1_ready = sems("rows1_ready")
        turned1 = sems("turned1")
        cols1_ready = sems("cols1_ready")
        y_ready = sems("y_ready")
        y_kept = sems("y_kept")
        y_stored = sems("y_stored")
        normed = sem("normed")
        out_stored = sem("out_stored")
        block = ctx.enter_context(nc.Block())

        def tile(t):
            return bass.ds(t * F, F)

        @block.sync
        def _(sp):
            sp.dma_start(src_i[:], src.rearrange("(p c) -> p c", p=P)).then_inc(EDGES_IN, 16)
            sp.dma_start(dst_i[:], dst.rearrange("(p c) -> p c", p=P)).then_inc(EDGES_IN, 16)
            sp.dma_start(typ_i[:], etype.rearrange("(p c) -> p c", p=P)).then_inc(TYPES_IN, 16)
            sp.dma_start(w_sb[:], ew.rearrange("(p c) -> p c", p=P)).then_inc(TYPES_IN, 16)
            sp.dma_start(x_sb[:], x.rearrange("(t p) f -> p t f", p=P)).then_inc(X_IN, 16)
            sp.dma_start(w1s[:], w_self1).then_inc(W_IN, 16)
            sp.dma_start(w1n[:], w_neigh1).then_inc(W_IN, 16)
            sp.dma_start(w2[:, 0:F], w_neigh2[0:F, :]).then_inc(W_IN, 16)
            sp.dma_start(w2[:, F:2 * F], w_self2[0:F, :]).then_inc(W_IN, 16)
            sp.dma_start(w2t[:, 0:F], w_neigh2[F:H, :]).then_inc(W_IN, 16)
            sp.dma_start(w2t[:, F:2 * F], w_self2[F:H, :]).then_inc(W_IN, 16)
            sp.dma_start(b1a[:], b1[0:F].rearrange("(p a) -> p a", a=1)).then_inc(W_IN, 16)
            sp.dma_start(b1b[:], b1[F:H].rearrange("(p a) -> p a", a=1)).then_inc(W_IN, 16)
            sp.dma_start(b2r[:], b2.rearrange("(a f) -> a f", a=1).partition_broadcast(P)).then_inc(W_IN, 16)
            sp.dma_start(wr[:], w_rel.rearrange("r o i -> o r i")).then_inc(W_IN, 16)
            for k, v in enumerate((gamma, beta, run_mean, run_var)):
                sp.dma_start(bn[:, k, :], v.rearrange("(a f) -> a f", a=1).partition_broadcast(P)).then_inc(BN_IN, 16)
            with sp.Fori(0, DTRIPS) as i:
                for k in range(SLOTS):
                    sp.wait_ge(g_kept[k], i + 2)
                    sp.dma_start(g_table[bass.ds((i * SLOTS + k) * P, P), :], g_sb[:, bass.ds(i * SLOTS + k, 1), :].rearrange("p a f -> p (a f)")).then_inc(g_stored[k], 16)
            with sp.Fori(0, DTRIPS) as i:
                for k in range(SLOTS):
                    sp.wait_ge(y_kept[k], i + 2)
                    sp.dma_start(
                        y_table.rearrange("(r n) f -> n r f", r=R)[bass.ds((i * SLOTS + k) * P, P), :, :],
                        y_sb[:, bass.ds(i * SLOTS + k, 1), :].rearrange("p a (r f) -> p (a r) f", r=R)).then_inc(y_stored[k], 16)
            sp.wait_ge(normed, 2)
            sp.dma_start(out.rearrange("(t p) f -> p t f", p=P), x_sb[:]).then_inc(out_stored, 16)
            sp.wait_ge(out_stored, 16)

        @block.gpsimd
        def _(pool):
            nc.gpsimd.iota(node_iota[:], pattern=[[1, N]], base=0, channel_multiplier=0,
                           allow_small_or_imprecise_dtypes=True).then_inc(const_made, 1)
            nc.gpsimd.memset(eps[:], 1e-5)
            nc.gpsimd.memset(zeros[:], 0.0)
            nc.gpsimd.memset(ident[:], 0.0).then_inc(const_made, 1)
            pool.wait_ge(const_made, 2)
            nc.gpsimd.affine_select(out=ident[:], in_=ident[:], compare_op=ALU.not_equal, fill=1.0, base=0,
                                    pattern=[[-1, 128]], channel_multiplier=1).then_inc(ident_made, 1)
            for layer, table in enumerate((x, g_table, y_table)):
                if layer == 1:
                    for k in range(SLOTS):
                        pool.wait_ge(g_stored[k], 16 * DTRIPS)
                if layer == 2:
                    for k in range(SLOTS):
                        pool.wait_ge(y_stored[k], 16 * DTRIPS)
                with pool.Fori(layer * TRIPS, (layer + 1) * TRIPS) as i:
                    for k in range(SLOTS):
                        pool.wait_ge(idx_ready[k], i + 1)
                        pool.wait_ge(chunk_done[k], i + 1)
                        pool.sem_inc(issued, 1)
                        pool.indirect_dma_start(
                            out=feat[:, k, :], out_offset=None, in_=table,
                            in_offset=bass.IndirectOffsetOnAxis(ap=idx[:, k:k + 1], axis=0)).then_inc(landed[k], 16)

        @block.scalar
        def _(act):
            def feed(layer, rows):
                with act.Fori(0, TRIPS) as i:
                    for k in range(SLOTS):
                        act.wait_ge(chunk_done[k], i + 1 + TRIPS * layer)
                        nc.scalar.copy(idx[:, k:k + 1], rows[:, bass.ds(i * SLOTS + k, 1)]).then_inc(idx_ready[k], 1)

            for k in range(SLOTS):
                act.sem_inc(y_kept[k], 1)
            act.wait_ge(EDGES_IN, 32)
            feed(0, src_i)
            act.wait_ge(wr_turned, R)
            nc.scalar.copy(wrT[:].rearrange("p r f -> p (r f)"), acc[:, DEG:DEG + R * F]).then_inc(wr_kept, 1)
            act.wait_ge(X_IN, 16)
            act.wait_ge(W_IN, 160)
            act.wait_ge(mean_ready, 1)
            with act.Fori(0, DTRIPS) as i:
                for k in range(SLOTS):
                    act.wait_ge(turned[k], i + 1)
                    nc.scalar.copy(row_x[:, k, :], x_sb[:, bass.ds(i * SLOTS + k, 1), :])
                    nc.scalar.copy(row_m[:, k, :], mean_sb[:, bass.ds(i * SLOTS + k, 1), :]).then_inc(rows_ready[k], 1)
                for k in range(SLOTS):
                    act.wait_ge(turned[k], i + 2)
                    nc.scalar.copy(cols[:, k, :, 0:P], acc[:, k * BANK:k * BANK + 256].rearrange(
                        "p (a n) -> p a n", a=2)[:, :, 0:P]).then_inc(cols_ready[k], 1)
                for k in range(SLOTS):
                    act.wait_ge(h_ready[k], i + 1)
                    nc.scalar.activation(hT[:, k, :], acc[:, k * BANK + 256:k * BANK + 256 + P], ACT.Relu, bias=b1a[:])
                    nc.scalar.activation(hTt[:, k, :], acc[0:H2, k * BANK + 384:k * BANK + 384 + P], ACT.Relu,
                                         bias=b1b[:]).then_inc(relu_done[k], 1)
            feed(1, src_i)
            act.wait_ge(sqrt_wait, TILES)
            nc.scalar.activation(bn_s[:], bn[:, 3, :], ACT.Sqrt, bias=eps[0:P, :])
            nc.scalar.activation(rstd[:], mv[:, :, 1], ACT.Sqrt, bias=eps[0:P, :]).then_inc(sqrt_done, 1)
            act.wait_ge(x1_ready, 1)
            with act.Fori(0, DTRIPS) as i:
                for k in range(SLOTS):
                    act.wait_ge(turned1[k], i + 1)
                    nc.scalar.copy(row_x[:, k, :], x_sb[:, bass.ds(i * SLOTS + k, 1), :]).then_inc(rows1_ready[k], 1)
                for k in range(SLOTS):
                    act.wait_ge(turned1[k], i + 2)
                    nc.scalar.copy(cols[:, k, 0, 0:P], acc[:, k * BANK:k * BANK + P]).then_inc(cols1_ready[k], 1)
                for k in range(SLOTS):
                    act.wait_ge(y_ready[k], i + 1)
                    nc.scalar.copy(y_sb[:, bass.ds(i * SLOTS + k, 1), :], acc[0:P, k * BANK:k * BANK + R * F].rearrange(
                        "p (a f) -> p a f", a=1)).then_inc(y_kept[k], 1)
            feed(2, rel_i)
            act.wait_ge(sqrt_wait, 2 * TILES)
            nc.scalar.activation(rstd[:], mv[:, :, 1], ACT.Sqrt, bias=eps[0:P, :]).then_inc(sqrt_done, 1)

        @block.vector
        def _(dve):
            steps = [0]

            def step(instruction):
                steps[0] += 1
                instruction.then_inc(dve_step, 1)
                dve.wait_ge(dve_step, steps[0])

            V = nc.vector
            flat = "p t f -> p (t f)"
            for k in range(SLOTS):
                dve.sem_inc(g_kept[k], 1)
            dve.wait_ge(EDGES_IN, 32)
            dve.wait_ge(const_made, 1)
            step(V.tensor_copy(dst_f[:], dst_i[:]))
            step(V.tensor_scalar(dst_hi[:], dst_f[:], 0.5, 1.0 / P, ALU.add, ALU.mult))
            step(V.tensor_scalar(dst_hi[:], dst_hi[:], -0.5, ROUND, ALU.add, ALU.add))
            step(V.tensor_scalar(dst_hi[:], dst_hi[:], ROUND, None, ALU.subtract))
            step(V.scalar_tensor_tensor(out=dst_lo[:], in0=dst_hi[:], scalar=-float(P), in1=dst_f[:],
                                        op0=ALU.mult, op1=ALU.add))
            with dve.Fori(0, TRIPS) as i:
                for k in range(SLOTS):
                    c = bass.ds(i * SLOTS + k, 1)
                    dve.wait_ge(deg_used[k], i + 1)
                    V.tensor_scalar(lo_hot[:, k, :], node_iota[:, 0:P], dst_lo[:, c], None, ALU.is_equal)
                    V.tensor_scalar(hi_hot[:, k, :], node_iota[:, 0:TILES], dst_hi[:, c], None,
                                    ALU.is_equal).then_inc(deg_hot[k], 1)
            dve.wait_ge(TYPES_IN, 32)
            V.tensor_copy(src_f[:], src_i[:])
            step(V.tensor_copy(typ_f[:], typ_i[:]))
            V.scalar_tensor_tensor(out=rel_i[:], in0=typ_f[:], scalar=float(N), in1=src_f[:],
                                   op0=ALU.mult, op1=ALU.add)
            V.tensor_scalar(is_r1[:], typ_f[:], 1.0, None, ALU.is_equal)
            step(V.tensor_scalar(scale[:], w_sb[:], 1.0, 0.5, ALU.add, ALU.mult))
            step(V.scalar_tensor_tensor(out=scale[:], in0=scale[:], scalar=0.0, in1=is_r1[:], op0=ALU.add, op1=ALU.mult))
            step(V.tensor_scalar(is_r1[:], is_r1[:], -1.0, 1.0, ALU.mult, ALU.add))
            step(V.tensor_tensor(scale[:], scale[:], is_r1[:], ALU.add))
            dve.wait_ge(deg_ready, 1)
            V.tensor_copy(deg[:], acc[0:P, DEG:DEG + TILES])
            step(V.tensor_scalar(deg_inv[:], acc[0:P, DEG:DEG + TILES], 1.0, None, ALU.max))
            step(V.reciprocal(deg_inv[:], deg_inv[:]))
            step(V.tensor_scalar(deg[:], deg[:], 0.0, None, ALU.is_gt))
            V.tensor_tensor(deg_inv[:], deg_inv[:], deg[:], ALU.mult).then_inc(deg_kept, 1)
            dve.wait_ge(deg_kept, 1)

            def onehots(layer):
                with dve.Fori(0, TRIPS) as i:
                    for k in range(SLOTS):
                        c = bass.ds(i * SLOTS + k, 1)
                        dve.wait_ge(chunk_done[k], i + 1 + TRIPS * layer)
                        if layer == 2:
                            V.tensor_scalar(onehot[:, k, :], node_iota[:], dst_f[:, c], scale[:, c], ALU.is_equal,
                                            ALU.mult).then_inc(onehot_ready[k], 1)
                        else:
                            V.tensor_scalar(onehot[:, k, :], node_iota[:], dst_f[:, c], None,
                                            ALU.is_equal).then_inc(onehot_ready[k], 1)

            def summed(layer):
                for k in range(SLOTS):
                    dve.wait_ge(chunk_done[k], TRIPS * (layer + 1) + 1)

            sums = acc[0:P, 0:ACC].rearrange("p (t f) -> p t f", f=F)
            inv_bc = deg_inv[:].rearrange("p (t a) -> p t a", a=1).broadcast_to([P, TILES, F])

            def layer_norm(rows, n):
                with dve.Fori(0, TILES) as t:
                    V.bn_stats(stats[:, bass.ds(t, 1), :], rows[:, bass.ds(t, 1), :]).then_inc(stats_made, 1)
                dve.wait_ge(stats_made, n * TILES)
                for t in range(TILES):
                    V.bn_aggr(mv[:, t, :], stats[:, t, :]).then_inc(sqrt_wait, 1)
                dve.wait_ge(sqrt_done, n)
                step(V.reciprocal(rstd[:], rstd[:]))
                mean = mv[:, :, 0:1].broadcast_to([P, TILES, F])
                step(V.tensor_tensor(rows[:], rows[:], mean, ALU.subtract))
                r = rstd[:].rearrange("p (t a) -> p t a", a=1).broadcast_to([P, TILES, F])
                V.tensor_tensor(x_sb[:], rows[:], r, ALU.mult).then_inc(normed, 1)
                dve.wait_ge(normed, n)

            onehots(0)
            summed(0)
            V.tensor_tensor(mean_sb[:], sums, inv_bc, ALU.mult).then_inc(mean_ready, 1)
            dve.wait_ge(X_IN, 16)
            dve.wait_ge(W_IN, 160)
            b2_bc = b2r[:].rearrange("p (a f) -> p a f", a=1).broadcast_to([P, TILES, F])
            step(V.tensor_tensor(self_sb[:], x_sb[:], b2_bc, ALU.add))
            with dve.Fori(0, DTRIPS) as i:
                for k in range(SLOTS):
                    dve.wait_ge(g_ready[k], i + 1)
                    t = bass.ds(i * SLOTS + k, 1)
                    V.tensor_tensor(self_sb[:, t, :], self_sb[:, t, :],
                                    acc[0:P, k * BANK + F:k * BANK + 2 * F].rearrange("p (a f) -> p a f", a=1), ALU.add)
                    V.tensor_copy(g_sb[:, t, :], acc[0:P, k * BANK:k * BANK + F].rearrange("p (a f) -> p a f", a=1)).then_inc(g_kept[k], 1)
            onehots(1)
            summed(1)
            step(V.tensor_tensor(mean_sb[:], sums, inv_bc, ALU.mult))
            step(V.tensor_tensor(mean_sb[:], mean_sb[:], self_sb[:], ALU.add))
            dve.wait_ge(BN_IN, 64)
            layer_norm(mean_sb, 1)
            step(V.reciprocal(bn_s[:], bn_s[:]))
            step(V.tensor_tensor(bn_a[:], bn_s[:], bn[:, 0, :], ALU.mult))
            step(V.tensor_tensor(bn_b[:], bn_a[:], bn[:, 2, :], ALU.mult))
            V.tensor_tensor(bn_b[:], bn[:, 1, :], bn_b[:], ALU.subtract).then_inc(x1_ready, 1)
            dve.wait_ge(x1_ready, 1)
            for k in range(SLOTS):
                dve.wait_ge(y_stored[k], 16 * DTRIPS)
            onehots(2)
            summed(2)
            step(V.tensor_tensor(mean_sb[:], sums, x_sb[:], ALU.add))
            bc = lambda v: v[:].rearrange("p (a f) -> p a f", a=1).broadcast_to([P, TILES, F])
            step(V.tensor_tensor(mean_sb[:], mean_sb[:], bc(bn_a), ALU.mult))
            step(V.tensor_tensor(mean_sb[:], mean_sb[:], bc(bn_b), ALU.add))
            step(V.scalar_tensor_tensor(out=mean_sb[:].rearrange(flat), in0=mean_sb[:].rearrange(flat), scalar=0.0,
                                        in1=x_sb[:].rearrange(flat), op0=ALU.max, op1=ALU.add))
            layer_norm(mean_sb, 2)

        @block.tensor
        def _(pe):
            mm = nc.tensor.matmul

            def clear(b, width=BANK):
                mm(acc[0:P, b * BANK:b * BANK + width], zeros[:], node_iota[:, 0:width], start=True, stop=False,
                   skip_group_check=True)

            for k in range(SLOTS):
                for credit in (chunk_done, deg_used, turned, turned1):
                    pe.sem_inc(credit[k], 1)
            pe.wait_ge(ident_made, 1)
            clear(BANKS)
            with pe.Fori(0, TRIPS) as i:
                for k in range(SLOTS):
                    pe.wait_ge(deg_hot[k], i + 1)
                    mm(acc[0:P, DEG:DEG + TILES], lo_hot[:, k, :], hi_hot[:, k, :], start=False, stop=False,
                       skip_group_check=True).then_inc(deg_used[k], 1)
            for k in range(SLOTS):
                pe.wait_ge(deg_used[k], TRIPS + 1)
            nc.tensor.nop().then_inc(deg_ready, 1)

            def aggregate(layer):
                for b in range(BANKS):
                    clear(b)
                with pe.Fori(layer * TRIPS, (layer + 1) * TRIPS) as i:
                    for k in range(SLOTS):
                        pe.wait_ge(landed[k], 16 * i + 16)
                        pe.wait_ge(onehot_ready[k], i + 1)
                        for t in range(TILES):
                            last = mm(acc[0:P, t * F:(t + 1) * F], onehot[:, k, t * P:(t + 1) * P], feat[:, k, :],
                                      start=False, stop=False, skip_group_check=True)
                        last.then_inc(chunk_done[k], 1)

            pe.wait_ge(deg_kept, 1)
            aggregate(0)
            pe.wait_ge(W_IN, 160)
            for r in range(R):
                nc.tensor.transpose(acc[:, DEG + r * F:DEG + (r + 1) * F], wr[:, r, :], ident[:]).then_inc(wr_turned, 1)
            pe.wait_ge(mean_ready, 1)
            with pe.Fori(0, DTRIPS) as i:
                for k in range(SLOTS):
                    pe.wait_ge(rows_ready[k], i + 1)
                    pe.wait_ge(g_kept[k], i + 1)
                    nc.tensor.transpose(acc[:, k * BANK:k * BANK + P], row_x[:, k, :], ident[0:P, 0:P])
                    nc.tensor.transpose(acc[:, k * BANK + 128:k * BANK + 128 + P], row_m[:, k, :],
                                        ident[0:P, 0:P]).then_inc(turned[k], 1)
                for k in range(SLOTS):
                    pe.wait_ge(cols_ready[k], i + 1)
                    o = k * BANK + 256
                    mm(acc[:, o:o + P], w1s[:, 0:F], cols[:, k, 0, 0:P], start=True, stop=False)
                    mm(acc[:, o:o + P], w1n[:, 0:F], cols[:, k, 1, 0:P], start=False, stop=True)
                    mm(acc[0:H2, o + 128:o + 128 + P], w1s[:, F:H], cols[:, k, 0, 0:P], start=True, stop=False)
                    mm(acc[0:H2, o + 128:o + 128 + P], w1n[:, F:H], cols[:, k, 1, 0:P], start=False,
                       stop=True).then_inc(h_ready[k], 1)
                for k in range(SLOTS):
                    pe.wait_ge(relu_done[k], i + 1)
                    mm(acc[0:P, k * BANK:k * BANK + 2 * F], hT[:, k, :], w2[:], start=True, stop=False)
                    mm(acc[0:P, k * BANK:k * BANK + 2 * F], hTt[:, k, :], w2t[:], start=False,
                       stop=True).then_inc(g_ready[k], 1)
            for k in range(SLOTS):
                pe.wait_ge(g_kept[k], DTRIPS + 1)
            aggregate(1)
            pe.wait_ge(wr_kept, 1)
            with pe.Fori(0, DTRIPS) as i:
                for k in range(SLOTS):
                    pe.wait_ge(rows1_ready[k], i + 1)
                    pe.wait_ge(y_kept[k], i + 1)
                    nc.tensor.transpose(acc[:, k * BANK:k * BANK + P], row_x[:, k, :],
                                        ident[0:P, 0:P]).then_inc(turned1[k], 1)
                for k in range(SLOTS):
                    pe.wait_ge(cols1_ready[k], i + 1)
                    mm(acc[0:P, k * BANK:k * BANK + R * F], cols[:, k, 0, 0:P], wrT[:].rearrange("p r f -> p (r f)"),
                       start=True, stop=True).then_inc(y_ready[k], 1)
            for k in range(SLOTS):
                pe.wait_ge(y_kept[k], DTRIPS + 1)
            aggregate(2)


_INS = ["x", "src", "dst", "edge_type_3", "edge_weight", "L0_gnn_W_self1", "L0_gnn_W_neigh1", "L0_gnn_b1",
        "L0_gnn_W_self2", "L0_gnn_W_neigh2", "L0_gnn_b2", "L1_gnn_W", "L1_gnn_gamma", "L1_gnn_beta",
        "L1_gnn_running_mean", "L1_gnn_running_var"]


def kernel(**inputs):
    import numpy as np
    import concourse.bacc as bacc
    from concourse.bass_utils import run_bass_kernel_spmd

    nc = bacc.Bacc("TRN2", target_bir_lowering=False, num_devices=1)
    arrays, args = {}, []
    for name in _INS:
        a = np.ascontiguousarray(inputs[name])
        arrays[f"in_{name}"] = a
        args.append(nc.dram_tensor(f"in_{name}", a.shape, mybir.dt.from_np(a.dtype), kind="ExternalInput").ap())
    out = nc.dram_tensor("out", arrays["in_x"].shape, F32, kind="ExternalOutput").ap()
    gnn_block(nc, *args, out)
    r = run_bass_kernel_spmd(nc, [arrays], core_ids=[0])
    return r.results[0]["out"]
```

```python
from contextlib import ExitStack

import numpy as np
import concourse.bass as bass
from concourse import mybir

F32 = mybir.dt.float32
F16 = mybir.dt.float16
BF16 = mybir.dt.bfloat16
I32 = mybir.dt.int32
ALU = mybir.AluOpType
ACT = mybir.ActivationFunctionType
AX = mybir.AxisListType

P = 125
SLOTS = 5
BANK = 512
ROUND = 12582912.0
J = 18
JP = J + J % 2
ROWS = 128
WINDOW_SHARES = (9, 18)
SIGNS = 12
DEPTH = 4
TYPE_STEP = 128
WEIGHT_SCALE = 64.0
BUILD_BANKS = 3
LAG = 2
RANKS = 128
X_LIMIT, WEIGHT_LIMIT, BIAS_LIMIT, EDGE_LIMIT = 32.0, 0.2, 16.0, 500.0
LOW = 2048.0


def gnn_block(nc, x, edges, ew, w_self1, w_neigh1, b1, w_self2, w_neigh2, b2,
              w_rel, gamma, beta, run_mean, run_var, out):
    E = edges.shape[1]
    src, dst, etype = (edges[k, 0:E] for k in range(3))
    N, F = x.shape
    H = w_self1.shape[1]
    R = w_rel.shape[0]
    LISTS = edges.shape[0]
    GATHERED, HIGH, LOWER, FULL, DENSE = (k * BANK for k in (3, 4, 5, 6, 7))
    TILES, CHUNKS = N // P, E // P
    H2 = H - F
    TRIPS = CHUNKS // SLOTS
    DTRIPS = TILES // SLOTS
    ACC = TILES * F
    BANKS = -(-ACC // BANK)
    WINDOW = ROWS * J
    COLS = TILES * J
    KEYS = TILES + 1
    BUCKETS = KEYS * TILES
    HALF = BUCKETS // 2
    RING = KEYS // 2
    PAIRS = TILES // 2
    XW = 2 * F + 2
    FIELDS = 4
    PLACE_WORDS = P * KEYS // 2
    SLOT_WORDS = PLACE_WORDS + TILES * FIELDS * KEYS // 2
    SPLIT = (14, KEYS - 14)
    GROUPS = -(-TILES // 4)
    assert N == TILES * P and E == CHUNKS * P and TRIPS * SLOTS == CHUNKS and DTRIPS * SLOTS == TILES
    assert H * WEIGHT_LIMIT * (2 * F * X_LIMIT * WEIGHT_LIMIT + BIAS_LIMIT) < 65504
    assert KEYS * J <= BANK and HALF <= BANK and KEYS % 2 == 0

    with ExitStack() as ctx:
        def sb(name, shape, dt=F32):
            return ctx.enter_context(nc.sbuf_tensor(name, shape, dt))

        def sem(name):
            return ctx.enter_context(nc.semaphore(name))

        def sems(name, n=SLOTS):
            return [sem(f"{name}{k}") for k in range(n)]

        def region(name, size):
            size = -(-size // 4) * 4
            whole = sb(name, [128, size // 4])

            def cutter(start=0):
                at = [start]

                def cut(shape, dt=F32):
                    n = 1
                    for d in shape[1:]:
                        n *= d
                    words = -(-n * mybir.dt.size(dt) // 4)
                    assert at[0] + words <= size // 4, (name, shape)
                    ap = whole[0:shape[0], at[0]:at[0] + words]
                    at[0] += words
                    if dt != F32:
                        ap = ap.bitcast(dt)
                    ap = ap[:, 0:n]
                    if len(shape) == 3:
                        ap = ap.rearrange("p (a b) -> p a b", b=shape[2])
                    if len(shape) == 4:
                        ap = ap.rearrange("p (a b c) -> p a b c", b=shape[2], c=shape[3])
                    return ap
                return cut
            return cutter

        g_table = nc.dram_tensor("g_table", (N, F), F32).ap()
        y_table = nc.dram_tensor("y_table", (R * N, F), F32).ap()
        rows_dram = nc.dram_tensor("rows_dram", (ROWS, COLS), I32).ap()
        slots_dram = nc.dram_tensor("slots_dram", (RANKS, SLOT_WORDS), F32).ap()
        scales_dram = nc.dram_tensor("scales_dram", (ROWS, 2 * COLS), F32).ap()

        ps = ctx.enter_context(nc.psum_tensor("ps", [128, 8 * BANK], F32))
        acc = ps
        DEG = BANKS * BANK

        x_sb = sb("x_sb", [P, TILES, F])
        w1s = sb("w1s", [F, H])
        w1n = sb("w1n", [F, H])
        w2 = sb("w2", [F, 2 * F])
        w2t = sb("w2t", [H2, 2 * F])
        b1a = sb("b1a", [F, 1])
        b1b = sb("b1b", [H2, 1])
        b2r = sb("b2r", [P, F])
        ident = sb("ident", [128, 128])
        eps = sb("eps", [128, 1])
        deg_inv = sb("deg_inv", [P, TILES])
        self_count = sb("self_count", [P, TILES])
        self_inv = sb("self_inv", [P, TILES])
        start_i = sb("start_i", [1, TILES], I32)
        flag_i = sb("flag_i", [1, 1], I32)
        flag_f = sb("flag_f", [1, 5])
        stats = sb("stats", [P, SLOTS, 6])
        mv = sb("mv", [P, SLOTS, 2])
        rstd = sb("rstd", [P, SLOTS])

        big = region("big", TILES * N * 2)
        features = region("features", TILES * XW * 2)
        pairs = region("pairs", 13056)
        slots = region("slots", 11704)

        adj = big()([P, TILES, TILES * P], BF16)
        xhl = features()([P, TILES, XW], F16)
        ghl = pairs()([P, TILES, 2 * F], F16)

        cut = big()
        dst_all = cut([P, CHUNKS], I32)
        before_lim = cut([P, TILES])
        below = cut([P, CHUNKS])
        signs = cut([P, CHUNKS])
        sign_sums = cut([P, SIGNS])
        tile_limits = cut([P, SIGNS])
        win = cut([ROWS, LISTS, COLS], I32)
        win_w = cut([ROWS, TILES, J])
        bucket = cut([ROWS, KEYS, COLS], F16)
        before = cut([ROWS, KEYS, COLS], F16)
        bucket_of = cut([ROWS, COLS + 1], F16)[:, 0:COLS]
        rank_iota = cut([ROWS, RANKS, JP], F16)
        rank_hot = cut([ROWS, SLOTS, RANKS * JP], F16)
        rank = cut([ROWS, TILES, JP], F16)
        values = cut([ROWS, FIELDS, COLS], F16)
        record = cut([ROWS, SLOTS, FIELDS * KEYS * JP], F16)
        lower = cut([ROWS, ROWS], F16)
        ident_h = cut([ROWS, ROWS], F16)
        ones_h = cut([ROWS, ROWS], F16)
        ones_f = cut([P, 1])
        outside_h = cut([128, 16], F16)
        ones_all = cut([128, 1], F16)
        flag_row = cut([1, 2, HALF])
        outside = cut([128, 16])
        src_n, dst_n, src_hi, src_lo, dst_hi, dst_lo, tile_of, is_in, is_self, typ_n, is_r1 = (
            cut([ROWS, COLS]) for _ in range(11))
        rel_row = cut([ROWS, COLS], I32)
        cut = pairs()
        both_hot = [cut([RANKS, 2, P * w], BF16) for w in SPLIT]
        src_hot, dst_hot = ([v[:, f, :] for v in both_hot] for f in range(2))
        cut = slots()
        place_iota = [cut([RANKS, P, w], F16) for w in SPLIT]
        buckets = cut([RANKS, TILES, FIELDS * KEYS], F16)
        type_part = pairs(P * (2 * SPLIT[0] + SPLIT[1]) // 2)([RANKS, TILES, KEYS], F16)
        slots_saved_part = slots()([RANKS, SLOT_WORDS])
        x_low = pairs()([P, TILES * F])
        is_out = pairs()([128, TILES * F])
        cut = slots()
        row_x = cut([128, SLOTS, F])
        row_m = cut([128, SLOTS, F])
        cols = cut([F, SLOTS, 2 * 128])
        low = cut([P, 2, F])
        ones_r = sb("ones_r", [RANKS, 1], BF16)

        cut = features()
        y_slot = cut([P, SLOTS, R * F])
        wr = cut([F, R * F])
        wrT = cut([F, R * F])
        cut = big()
        x1hl = cut([P, TILES, 2 * F], F16)
        rows_in = cut([ROWS, COLS], I32)
        scales_in = cut([ROWS, 2 * COLS])
        slots_in = cut([RANKS, SLOT_WORDS])
        bn = cut([P, 4, F])
        FREED = -(-(TILES * F + 3 * COLS + SLOT_WORDS + 4 * F) * 4 // (N * 2))
        bn_s = cut([P, F])
        bn_a = cut([P, F])
        bn_b = cut([P, F])
        idx_t = cut([ROWS, 2, J], I32)
        feat_t = cut([ROWS, 2, J * F])
        dst_t = cut([ROWS, 2, J * P])
        place_f = cut([ROWS, P])
        z_t = cut([P, 2, F])
        result = cut([P, TILES, F])
        places = [slots_in[:, a * P // 2:(a + w) * P // 2].bitcast(F16).rearrange("p (n b) -> p n b", b=w)
                  for a, w in ((0, SPLIT[0]), (SPLIT[0], SPLIT[1]))]
        records = slots_in[:, KEYS * P // 2:SLOT_WORDS].bitcast(F16).rearrange("p (t g) -> p t g", g=FIELDS * KEYS)
        place_typ = [None, cut([RANKS, TILES, KEYS], F16), cut([RANKS, TILES, KEYS], F16)]
        hots = [cut([RANKS, 5, P * w], F16) for w in SPLIT]
        x1_self = cut([P, 2, F])
        a02 = cut([P, RING, 2 * P], F16)
        a1 = cut([P, RING, P])
        sum_high = cut([F, 2 * P])
        dense_sums = cut([F, 3, P])

        cut = big()
        g_mean_sb = cut([P, TILES, F])
        g_self_sb = cut([P, TILES, F])
        g_src_i, g_dst_i, g_typ_i, g_rel_i = (cut([P, CHUNKS], I32) for _ in range(4))
        g_dst_f, g_dst_hi, g_dst_lo, g_src_f, g_typ_f, g_is_r1, g_w_sb, g_scale = (cut([P, CHUNKS]) for _ in range(8))
        g_node_iota = cut([P, N])
        g_zeros = cut([P, P])
        g_idx = cut([P, SLOTS], I32)
        g_feat = cut([P, SLOTS, F])
        g_onehot = cut([P, SLOTS, N])
        cut = slots()
        g_row_x = cut([P, SLOTS, F])
        g_row_m = cut([P, SLOTS, F])
        g_cols = cut([F, SLOTS, 2, 128])
        cut = features()
        g_g_sb = cut([P, TILES, F])
        cut = pairs()
        g_wr = cut([F, R, F])
        g_wrT = cut([F, R, F])
        g_bn = cut([P, 4, F])
        g_bn_a, g_bn_b, g_bn_s = (cut([P, F]) for _ in range(3))
        g_stats = cut([P, TILES, 6])
        g_mv = cut([P, TILES, 2])
        g_rstd = cut([P, TILES])
        g_deg = cut([P, TILES])
        g_hi_hot = cut([P, SLOTS, TILES])
        cut = big(2 * TILES * F + 12 * CHUNKS + N + P + SLOTS * (1 + F))
        g_y_sb = cut([P, TILES, R * F])
        g_lo_hot = cut([P, SLOTS, P])
        any_hT = cut([F, SLOTS, P])
        any_hTt = cut([H2, SLOTS, P])

        DST_IN, X_IN, W_IN, WINW_IN = (sem(n) for n in ("DST_IN", "X_IN", "W_IN", "WINW_IN"))
        WIN_IN = sems("WIN_IN", 3)
        consts = sem("consts")
        ident_made = sem("ident_made")
        dve_step = sem("dve_step")
        starts_counted = sem("starts_counted")
        limits_made, signs_summed = sem("limits_made"), sem("signs_summed")
        limits_checked, limits_summed = sem("limits_checked"), sem("limits_summed")
        starts_summed = sem("starts_summed")
        starts_ready = sem("starts_ready")
        buckets_marked = sem("buckets_marked")
        prefixes_counted = sem("prefixes_counted")
        buckets_counted = sem("buckets_counted")
        flag_ready = sem("flag_ready")
        rows_saved = sem("rows_saved")
        numbers_ready = sem("numbers_ready")
        ranks_parts = sem("ranks_parts")
        ranks_summed = sem("ranks_summed")
        rank_hot_ready = sem("rank_hot_ready")
        sorted_out = sem("sorted_out")
        sorted_kept = sem("sorted_kept")
        hots_ready = sems("hots_ready", 2)
        first_used = sem("first_used")
        blocks_ready = sem("blocks_ready")
        blocks_kept = sem("blocks_kept")
        self_ready = sem("self_ready")
        self_kept = sem("self_kept")
        high_ready = sem("high_ready")
        pairs_ready = sem("pairs_ready")
        sums_ready = sem("sums_ready")
        mean_ready = sem("mean_ready")
        row_ready = sem("row_ready")
        turned = sem("turned")
        cols_ready = sem("cols_ready")
        h_ready = sem("h_ready")
        relu_done = sem("relu_done")
        g_ready = sem("g_ready")
        g_high = sem("g_high")
        bank_free = sem("bank_free")
        g_pairs = sem("g_pairs")
        WR_IN, L1_IN, BN_IN = sem("WR_IN"), sem("L1_IN"), sem("BN_IN")
        wr_turned = sem("wr_turned")
        wr_kept = sem("wr_kept")
        sums2_ready = sem("sums2_ready")
        var2_ready = sem("var2_ready")
        root2_ready = sem("root2_ready")
        x1_ready = sem("x1_ready")
        x1_kept = sem("x1_kept")
        turned2 = sem("turned2")
        cols2_ready = sem("cols2_ready")
        y_ready = sem("y_ready")
        y_kept = sem("y_kept")
        y_stored = sems("y_stored")
        place_made = sem("place_made")
        idx_ready = sem("idx_ready")
        landed = sems("landed")
        issued = sem("issued")
        dst_ready = sem("dst_ready")
        tile_done = sem("tile_done")
        low_step = sem("low_step")
        x1_pairs = sem("x1_pairs")
        hots_made = sems("hots_made", 2)
        block_built = sem("block_built")
        block_kept = sem("block_kept")
        block_used = sem("block_used")
        self_copied = sem("self_copied")
        sums_copied = sem("sums_copied")
        sums_joined = sem("sums_joined")
        dense_done = sem("dense_done")
        acc_read = sem("acc_read")
        dense_read = sem("dense_read")
        slots_saved = sem("slots_saved")
        bn_root = sem("bn_root")
        var3_ready = sem("var3_ready")
        root3_ready = sem("root3_ready")
        out_ready = sem("out_ready")
        out_stored = sems("out_stored")
        conv_step, self_step, conv2_step, norm_step = (sem(n) for n in ("conv_step", "self_step", "conv2_step", "norm_step"))
        root_inv = sem("root_inv")
        root_inv3 = sem("root_inv3")
        hot1_step = sem("hot1_step")
        wait_taken = sem("wait_taken")
        EDGES_IN, TYPES_IN, any_BN_IN = sem("EDGES_IN"), sem("TYPES_IN"), sem("any_BN_IN")
        any_dve_step = sem("any_dve_step")
        any_idx_ready = idx_ready
        any_landed = landed
        any_onehot_ready = dst_ready
        any_chunk_done = tile_done
        any_issued = issued
        any_deg_ready = sem("any_deg_ready")
        any_deg_hot = rank_hot_ready
        any_deg_used = sorted_out
        any_wr_turned = wr_turned
        any_wr_kept = wr_kept
        any_deg_kept = sem("any_deg_kept")
        any_mean_ready = sem("any_mean_ready")
        any_rows_ready = row_ready
        any_turned = turned
        any_cols_ready = cols_ready
        any_h_ready = h_ready
        any_relu_done = relu_done
        any_g_ready = g_ready
        any_g_kept = bank_free
        any_g_stored = out_stored
        any_x1_ready = sem("any_x1_ready")
        any_sqrt_wait = sem("any_sqrt_wait")
        any_stats_made = sem("any_stats_made")
        any_sqrt_done = sem("any_sqrt_done")
        any_rows1_ready = x1_ready
        any_turned1 = turned2
        any_cols1_ready = cols2_ready
        any_y_ready = y_ready
        any_y_kept = y_kept
        any_y_stored = y_stored
        any_normed = sem("any_normed")
        any_out_stored = sem("any_out_stored")
        any_const_made = sem("any_const_made")
        block = ctx.enter_context(nc.Block())

        def bank(k, a=0, b=BANK):
            return ps[:, k * BANK + a:k * BANK + b]

        def nth(trip, k):
            return trip * SLOTS + (k + 1 - SLOTS)

        def one(t):
            return bass.ds(t, 1)

        def conv_bank(k, a=0, b=BANK):
            return bank(k + 1, a, b)

        def pipeline(eng, step, peeled=1):
            def trip(i, first=False, last=False):
                for k in range(SLOTS + (DEPTH if last else 0)):
                    back = lambda d, k=k: (i * SLOTS + (k - d), (k - d) % SLOTS, i + (k - d) // SLOTS)
                    has = lambda d, k=k: (not first or k - d >= 0) and (not last or k - d < SLOTS)
                    step(back, has)

            trip(0, first=True)
            for i in range(1, peeled):
                trip(i)
            with eng.Fori(peeled, DTRIPS - 1) as i:
                trip(i)
            trip(DTRIPS - 1, last=True)

        def previous_use(b, ring):
            return b - ring + 1 if b >= ring else max(c for c in range(KEYS) if c % ring == b) - KEYS + 1

        def window_loads(eng, queue, first, end):
            eng.wait_ge(starts_ready, 1)
            def window(t, start):
                eng.dma_start(win[:, :, bass.ds(t * J, J)],
                              edges[:, bass.ds(start, WINDOW)].rearrange("a (p j) -> p a j", j=J)).then_inc(WIN_IN[queue], 16)

            at = lambda t: eng.value_load(start_i[0:1, one(t)], min_val=0, max_val=E - WINDOW)
            triples = (end - first) // 3
            with eng.Fori(0, triples) as i:
                for t, start in [(i * 3 + (first + n), at(i * 3 + (first + n))) for n in range(3)]:
                    window(t, start)
            for t in range(first + 3 * triples, end):
                window(t, at(t))

        @block.sync
        def _(sp):

            sp.dma_start(dst_all, dst.rearrange("(p c) -> p c", p=P)).then_inc(DST_IN, 16)
            sp.dma_start(x_sb[:], x.rearrange("(t p) f -> p t f", p=P)).then_inc(X_IN, 16)
            window_loads(sp, 0, 0, WINDOW_SHARES[0])
            sp.dma_start(w1s[:], w_self1).then_inc(W_IN, 16)
            sp.dma_start(w1n[:], w_neigh1).then_inc(W_IN, 16)
            sp.dma_start(w2[:, 0:F], w_neigh2[0:F, :]).then_inc(W_IN, 16)
            sp.dma_start(w2[:, F:2 * F], w_self2[0:F, :]).then_inc(W_IN, 16)
            sp.dma_start(w2t[:, 0:F], w_neigh2[F:H, :]).then_inc(W_IN, 16)
            sp.dma_start(w2t[:, F:2 * F], w_self2[F:H, :]).then_inc(W_IN, 16)
            sp.dma_start(b1a[:], b1[0:F].rearrange("(p a) -> p a", a=1)).then_inc(W_IN, 16)
            sp.dma_start(b1b[:], b1[F:H].rearrange("(p a) -> p a", a=1)).then_inc(W_IN, 16)
            sp.dma_start(b2r[:], b2.rearrange("(a f) -> a f", a=1).partition_broadcast(P)).then_inc(W_IN, 16)

            sp.wait_ge(flag_ready, 1)
            fits = sp.value_load(flag_i[0:1, 0:1], min_val=0, max_val=1)
            with sp.If(fits):

                sp.wait_ge(numbers_ready, 1)
                sp.dma_start(rows_dram, rel_row).then_inc(rows_saved, 16)
                sp.dma_start(scales_dram[:, 0:COLS], dst_lo).then_inc(rows_saved, 16)
                sp.dma_start(scales_dram[:, COLS:2 * COLS], src_n).then_inc(rows_saved, 16)
                sp.wait_ge(ident_made, 4)
                sp.dma_start(slots_dram[:, 0:PLACE_WORDS], slots_saved_part[:, 0:PLACE_WORDS]).then_inc(slots_saved, 16)
                sp.wait_ge(sorted_kept, nth(DTRIPS + 1, SLOTS - 1))
                sp.dma_start(slots_dram[:, PLACE_WORDS:SLOT_WORDS],
                             slots_saved_part[:, PLACE_WORDS:SLOT_WORDS]).then_inc(slots_saved, 16)
                sp.wait_ge(sums_ready, nth(DTRIPS, SLOTS - 1))
                sp.dma_start(wr.rearrange("o (r i) -> o r i", r=R), w_rel.rearrange("r o i -> o r i")).then_inc(WR_IN, 16)
                def store_rows(i):
                    for k in range(SLOTS):
                        sp.wait_ge(y_kept, nth(i + 2, k))
                        sp.dma_start(
                            y_table.rearrange("(r n) f -> n r f", r=R)[bass.ds((i * SLOTS + k) * P, P), :, :],
                            y_slot[:, k, :].rearrange("p (r f) -> p r f", r=R)).then_inc(y_stored[k], 16)

                with sp.Fori(0, DTRIPS - 2) as i:
                    store_rows(i)
                sp.wait_ge(sums2_ready, FREED)
                sp.wait_ge(rows_saved, 48)
                sp.wait_ge(slots_saved, 32)
                sp.dma_start(rows_in, rows_dram).then_inc(L1_IN, 16)
                sp.dma_start(scales_in, scales_dram).then_inc(L1_IN, 16)
                sp.dma_start(slots_in, slots_dram).then_inc(L1_IN, 16)
                for k, v in enumerate((gamma, beta, run_mean, run_var)):
                    sp.dma_start(bn[:, k, :], v.rearrange("(a f) -> a f", a=1).partition_broadcast(P)).then_inc(BN_IN, 16)
                for i in (DTRIPS - 2, DTRIPS - 1):
                    store_rows(i)
                nodes = out.rearrange("(t p) f -> p t f", p=P)
                with sp.Fori(0, PAIRS) as q:
                    sp.wait_ge(out_ready, q * 2 + 2)
                    sp.dma_start(nodes[:, bass.ds(q * 2, 2), :], result[:, bass.ds(q * 2, 2), :]).then_inc(out_stored[0], 16)
                sp.wait_ge(out_ready, TILES)
                sp.dma_start(nodes[:, TILES - 1, :], result[:, TILES - 1, :]).then_inc(out_stored[0], 16)
                sp.wait_ge(out_stored[0], 16 * (PAIRS + 1))

            with sp.Else():
                sp.dma_start(g_src_i[:], src.rearrange("(p c) -> p c", p=P)).then_inc(EDGES_IN, 16)
                sp.dma_start(g_dst_i[:], dst.rearrange("(p c) -> p c", p=P)).then_inc(EDGES_IN, 16)
                sp.dma_start(g_typ_i[:], etype.rearrange("(p c) -> p c", p=P)).then_inc(TYPES_IN, 16)
                sp.dma_start(g_w_sb[:], ew.rearrange("(p c) -> p c", p=P)).then_inc(TYPES_IN, 16)
                sp.dma_start(g_wr[:], w_rel.rearrange("r o i -> o r i")).then_inc(WR_IN, 16)
                for k, v in enumerate((gamma, beta, run_mean, run_var)):
                    sp.dma_start(g_bn[:, k, :], v.rearrange("(a f) -> a f", a=1).partition_broadcast(P)).then_inc(any_BN_IN, 16)
                with sp.Fori(0, DTRIPS) as i:
                    for k in range(SLOTS):
                        sp.wait_ge(any_g_kept, nth(i + 2, k))
                        sp.dma_start(
                            g_table[bass.ds((i * SLOTS + k) * P, P), :],
                            g_g_sb[:, one(i * SLOTS + k), :].rearrange("p a f -> p (a f)")).then_inc(any_g_stored[k], 16)
                with sp.Fori(0, DTRIPS) as i:
                    for k in range(SLOTS):
                        sp.wait_ge(any_y_kept, nth(i + 2, k))
                        sp.dma_start(
                            y_table.rearrange("(r n) f -> n r f", r=R)[bass.ds((i * SLOTS + k) * P, P), :, :],
                            g_y_sb[:, one(i * SLOTS + k), :].rearrange(
                                "p a (r f) -> p (a r) f", r=R)).then_inc(any_y_stored[k], 16)
                sp.wait_ge(any_normed, 2)
                sp.dma_start(out.rearrange("(t p) f -> p t f", p=P), x_sb[:]).then_inc(any_out_stored, 16)
                sp.wait_ge(any_out_stored, 16)

        @block.gpsimd
        def _(pool):

            def iota(out_ap, pattern, base=0):
                return nc.gpsimd.iota(out_ap, pattern=pattern, base=base, channel_multiplier=0,
                                      allow_small_or_imprecise_dtypes=True)

            iota(tile_limits, [[-P, SIGNS]]).then_inc(limits_made, 1)
            pool.wait_ge(limits_made, 1)
            nc.gpsimd.tensor_scalar(tile_limits, tile_limits, 0.5, None, ALU.add).then_inc(limits_made, 1)
            nc.gpsimd.memset(eps[:], 1e-5)
            nc.gpsimd.memset(ones_f, 1.0)
            nc.gpsimd.memset(ones_all, 1.0)
            nc.gpsimd.memset(ones_r[:], 1.0)
            nc.gpsimd.memset(ident_h, 0.0)
            nc.gpsimd.memset(ones_h, 1.0)
            nc.gpsimd.memset(lower, 1.0)
            nc.gpsimd.memset(xhl[:, :, 2 * F:XW], 1.0)
            nc.gpsimd.memset(ident[:], 0.0).then_inc(consts, 1)
            iota(tile_of.rearrange("p (t j) -> p t j", j=J), [[1, TILES], [0, J]]).then_inc(consts, 1)
            pool.wait_ge(consts, 2)
            nc.gpsimd.affine_select(out=ident[:], in_=ident[:], compare_op=ALU.not_equal, fill=1.0, base=0,
                                    pattern=[[-1, 128]], channel_multiplier=1)
            nc.gpsimd.affine_select(out=ident_h, in_=ident_h, compare_op=ALU.not_equal, fill=1.0, base=0,
                                    pattern=[[-1, ROWS]], channel_multiplier=1)
            nc.gpsimd.affine_select(out=lower, in_=lower, compare_op=ALU.is_gt, fill=0.0, base=0,
                                    pattern=[[1, ROWS]], channel_multiplier=-1).then_inc(ident_made, 1)
            window_loads(pool, 2, WINDOW_SHARES[1], TILES)
            with pool.Fori(0, TILES) as t:
                start = pool.value_load(start_i[0:1, one(t)], min_val=0, max_val=E - WINDOW)
                pool.dma_start(win_w[:, one(t), :].rearrange("p a j -> p (a j)"),
                               ew[bass.ds(start, WINDOW)].rearrange("(p j) -> p j", j=J)).then_inc(WINW_IN, 16)
            iota(rank_iota, [[1, RANKS], [0, JP]]).then_inc(ident_made, 1)
            for v, w in zip(place_iota, SPLIT):
                iota(v, [[1, P], [0, w]], base=1).then_inc(ident_made, 1)

            pool.wait_ge(flag_ready, 1)
            fits = pool.value_load(flag_i[0:1, 0:1], min_val=0, max_val=1)
            with pool.If(fits):

                pool.wait_ge(sums2_ready, nth(DTRIPS, SLOTS - 1))
                iota(place_f, [[1, P]], base=1).then_inc(place_made, 1)
                for k in range(SLOTS):
                    pool.wait_ge(y_stored[k], 16 * DTRIPS)

                def gather(q, u, fresh):
                    pool.wait_ge(idx_ready, q + 1)
                    if not fresh:
                        pool.wait_ge(tile_done, q - 1)
                    pool.sem_inc(issued, 1)
                    for j in range(J):
                        pool.indirect_dma_start(
                            out=feat_t[:, u, j * F:(j + 1) * F], out_offset=None, in_=y_table,
                            in_offset=bass.IndirectOffsetOnAxis(ap=idx_t[:, u, j:j + 1], axis=0)).then_inc(landed[u], 16)

                for q in range(2):
                    gather(q, q, True)
                with pool.Fori(1, PAIRS // 2) as i:
                    for u in range(2):
                        gather(i * 2 + u, u, False)
                gather(PAIRS, 0, False)

            with pool.Else():
                nc.gpsimd.iota(g_node_iota[:], pattern=[[1, N]], base=0, channel_multiplier=0,
                               allow_small_or_imprecise_dtypes=True).then_inc(any_const_made, 1)
                nc.gpsimd.memset(g_zeros[:], 0.0).then_inc(any_const_made, 1)
                for layer, table in enumerate((x, g_table, y_table)):
                    if layer == 1:
                        for k in range(SLOTS):
                            pool.wait_ge(any_g_stored[k], 16 * DTRIPS)
                    if layer == 2:
                        for k in range(SLOTS):
                            pool.wait_ge(any_y_stored[k], 16 * DTRIPS)
                    with pool.Fori(layer * TRIPS, (layer + 1) * TRIPS) as i:
                        for k in range(SLOTS):
                            pool.wait_ge(any_idx_ready, nth(i + 1, k))
                            pool.wait_ge(any_chunk_done, nth(i + 1, k))
                            pool.sem_inc(any_issued, 1)
                            pool.indirect_dma_start(
                                out=g_feat[:, k, :], out_offset=None, in_=table,
                                in_offset=bass.IndirectOffsetOnAxis(ap=g_idx[:, k:k + 1], axis=0)).then_inc(any_landed[k], 16)

        @block.scalar
        def _(act):

            act.wait_ge(DST_IN, 16)
            act.wait_ge(limits_made, 2)
            for t in range(1, SIGNS):
                nc.scalar.activation(signs, dst_all, ACT.Sign, bias=tile_limits[:, t:t + 1],
                                     accum_out=sign_sums[:, t:t + 1]).then_inc(signs_summed, 1)
                act.wait_ge(signs_summed, t)
            act.wait_ge(X_IN, 16)
            act.wait_ge(consts, 1)
            nc.scalar.activation(xhl[:, :, 0:F], x_sb[:], ACT.Copy).then_inc(high_ready, 1)
            window_loads(act, 1, WINDOW_SHARES[0], WINDOW_SHARES[1])

            act.wait_ge(flag_ready, 1)
            fits = act.value_load(flag_i[0:1, 0:1], min_val=0, max_val=1)
            with act.If(fits):

                copy = lambda o, a: nc.scalar.activation(o, a, ACT.Copy)
                for k in range(SLOTS):
                    act.sem_inc(sorted_kept, 1)
                    act.sem_inc(y_kept, 1)
                act.sem_inc(blocks_kept, GROUPS)
                act.sem_inc(self_kept, 1)
                with act.Fori(0, DTRIPS) as i:
                    for k in range(SLOTS):
                        act.wait_ge(sorted_out, nth(i + 2, k))
                        copy(buckets[:, one(i * SLOTS + k), :],
                             ps[:, k * BANK:k * BANK + FIELDS * KEYS].rearrange("p (a f) -> p a f", a=1)).then_inc(sorted_kept, 1)
                act.wait_ge(rows_saved, 48)
                with act.Fori(0, TILES) as t:
                    for g in range(GROUPS):
                        n = min(4, TILES - 4 * g)
                        act.wait_ge(blocks_ready, t * GROUPS + g + 1)
                        copy(adj[:, one(t), 4 * g * P:(4 * g + n) * P],
                             ps[0:P, g * BANK:g * BANK + n * P].rearrange("p (a f) -> p a f", a=1)).then_inc(blocks_kept, 1)
                    act.wait_ge(self_ready, t + 2)
                    copy(self_count[:, one(t)], ps[0:P, 7 * BANK:7 * BANK + 1]).then_inc(self_kept, 1)
                act.wait_ge(W_IN, 16 * 9)
                act.wait_ge(slots_saved, 32)

                def first_conv(back, has):
                    if has(0):
                        t, k, _ = back(0)
                        act.wait_ge(g_ready, t + 1)
                        copy(row_x[0:P, k, :], x_sb[:, one(t), :].rearrange("p a f -> p (a f)")).then_inc(row_ready, 1)
                    if has(1):
                        t, k, _ = back(1)
                        act.wait_ge(turned, t + 1)
                        copy(cols[:, k, :].rearrange("p (a n) -> p a n", a=2)[:, :, 0:P],
                             conv_bank(k, 0, 256).rearrange("p (a n) -> p a n", a=2)[:, :, 0:P]).then_inc(cols_ready, 1)
                    if has(2):
                        t, k, _ = back(2)
                        act.wait_ge(h_ready, t + 1)
                        nc.scalar.activation(row_m[:, k, 0:P], conv_bank(k, 256, 256 + P), ACT.Relu, bias=b1a[:])
                        nc.scalar.activation(row_x[0:H2, k, 0:P], conv_bank(k, 384, 384 + P)[0:H2, :], ACT.Relu,
                                             bias=b1b[:]).then_inc(relu_done, 1)
                    if has(3):
                        t, k, _ = back(3)
                        act.wait_ge(g_ready, t + (SLOTS + 1))
                        copy(ghl[:, one(t), 0:F],
                             conv_bank(k, 0, F)[0:P, :].rearrange("p (a f) -> p a f", a=1)).then_inc(g_high, 1)

                pipeline(act, first_conv)
                act.wait_ge(wr_turned, R)
                copy(wrT, ps[:, 7 * BANK:7 * BANK + R * F]).then_inc(wr_kept, 1)

                def second_conv(back, has):
                    if has(0):
                        t, k, _ = back(0)
                        act.wait_ge(var2_ready, t + 1)
                        nc.scalar.activation(rstd[:, k:k + 1], mv[:, k, 1:2], ACT.Sqrt, bias=eps[0:P, :]).then_inc(root2_ready, 1)
                    if has(2):
                        t, k, _ = back(2)
                        act.wait_ge(x1_ready, t + 1)
                        copy(x_sb[:, one(t), :].rearrange("p a f -> p (a f)"), row_x[0:P, k, :])
                        copy(x1hl[:, one(t), 0:F].rearrange("p a f -> p (a f)"), row_x[0:P, k, :]).then_inc(x1_kept, 1)
                        act.wait_ge(turned2, t + 1)
                        copy(cols[:, k, 0:P], conv_bank(k, 384, 384 + P)).then_inc(cols2_ready, 1)
                    if has(3):
                        t, k, i = back(3)
                        act.wait_ge(y_ready, t + (SLOTS + 1))
                        if not isinstance(i, int) or i > 0:
                            act.wait_ge(y_stored[k], 16 * i)
                        copy(y_slot[:, k, :], conv_bank(k, 0, R * F)[0:P, :]).then_inc(y_kept, 1)

                pipeline(act, second_conv, peeled=2)
                act.wait_ge(L1_IN, 16 * 3)

                def feed(q, u, fresh):
                    if not fresh:
                        act.wait_ge(tile_done, q - 1)
                    copy(idx_t[:, u, :], rows_in[:, bass.ds(q * (2 * J), J)]).then_inc(idx_ready, 1)

                for q in range(2):
                    feed(q, q, True)
                act.wait_ge(BN_IN, 16 * 4)
                nc.scalar.activation(bn_s, bn[:, 3, :], ACT.Sqrt, bias=eps[0:P, :]).then_inc(bn_root, 1)

                def copy_sums(q, fresh):
                    act.wait_ge(block_used, q * KEYS + KEYS)
                    if not fresh:
                        act.wait_ge(dense_done, q)
                    copy(sum_high, ps[:, HIGH:HIGH + 2 * P])
                    nc.scalar.activation(dense_sums[:, 2, :], ps[:, FULL:FULL + P], ACT.Copy,
                                         scale=1.0 / WEIGHT_SCALE).then_inc(sums_copied, 1)

                def roots(q):
                    act.wait_ge(var3_ready, q * 2 + 2)
                    nc.scalar.activation(rstd[:, 0:2], mv[:, 0:2, 1], ACT.Sqrt, bias=eps[0:P, :]).then_inc(root3_ready, 1)

                def keep_blocks(q, u, first=False):
                    if not first:
                        copy_sums(q - 1, fresh=isinstance(q, int) and q == 1)
                        feed(q + 1, 1 - u, False)
                    copy(x1_self[:, u, :], x_sb[:, one(q * 2 + 1), :].rearrange("p a f -> p (a f)")).then_inc(self_copied, 1)
                    for b in range(KEYS):
                        act.wait_ge(block_built, q * KEYS + b + 1)
                        if not (first and b < RING):
                            act.wait_ge(block_used, q * KEYS + previous_use(b, RING))
                        at = b % RING
                        o = b % BUILD_BANKS * BANK
                        copy(a02[:, at, :], ps[0:P, o:o + 2 * P])
                        copy(a1[:, at, :], ps[0:P, o + 2 * P:o + 3 * P]).then_inc(block_kept, 1)
                        if b == 17 and not first:
                            roots(q - 1)

                keep_blocks(0, 0, first=True)
                keep_blocks(1, 1)
                with act.Fori(1, PAIRS // 2) as i:
                    for u in range(2):
                        keep_blocks(i * 2 + u, u)
                copy_sums(PAIRS - 1, False)
                roots(PAIRS - 1)
                act.wait_ge(var3_ready, TILES)
                nc.scalar.activation(rstd[:, 1:2], mv[:, 1, 1:2], ACT.Sqrt, bias=eps[0:P, :]).then_inc(root3_ready, 1)

            with act.Else():
                def feed(layer, rows):
                    with act.Fori(0, TRIPS) as i:
                        for k in range(SLOTS):
                            act.wait_ge(any_chunk_done, nth(i + 1 + TRIPS * layer, k))
                            nc.scalar.copy(g_idx[:, k:k + 1], rows[:, bass.ds(i * SLOTS + k, 1)]).then_inc(any_idx_ready, 1)

                for k in range(SLOTS):
                    act.sem_inc(any_y_kept, 1)
                act.wait_ge(EDGES_IN, 32)
                feed(0, g_src_i)
                act.wait_ge(any_wr_turned, R)
                nc.scalar.copy(g_wrT[:].rearrange("p r f -> p (r f)"), acc[:, DEG:DEG + R * F]).then_inc(any_wr_kept, 1)
                act.wait_ge(X_IN, 16)
                act.wait_ge(W_IN, 16 * 9)
                act.wait_ge(any_mean_ready, 1)
                with act.Fori(0, DTRIPS) as i:
                    for k in range(SLOTS):
                        act.wait_ge(any_turned, nth(i + 1, k))
                        nc.scalar.copy(g_row_x[:, k, :], x_sb[:, bass.ds(i * SLOTS + k, 1), :])
                        nc.scalar.copy(g_row_m[:, k, :], g_mean_sb[:, bass.ds(i * SLOTS + k, 1), :]).then_inc(any_rows_ready, 1)
                    for k in range(SLOTS):
                        act.wait_ge(any_turned, nth(i + 2, k))
                        nc.scalar.copy(g_cols[:, k, :, 0:P], acc[:, k * BANK:k * BANK + 256].rearrange(
                            "p (a n) -> p a n", a=2)[:, :, 0:P]).then_inc(any_cols_ready, 1)
                    for k in range(SLOTS):
                        act.wait_ge(any_h_ready, nth(i + 1, k))
                        nc.scalar.activation(any_hT[:, k, :], acc[:, k * BANK + 256:k * BANK + 256 + P], ACT.Relu, bias=b1a[:])
                        nc.scalar.activation(any_hTt[:, k, :], acc[0:H2, k * BANK + 384:k * BANK + 384 + P], ACT.Relu,
                                             bias=b1b[:]).then_inc(any_relu_done, 1)
                feed(1, g_src_i)
                act.wait_ge(any_sqrt_wait, TILES)
                nc.scalar.activation(g_bn_s[:], g_bn[:, 3, :], ACT.Sqrt, bias=eps[0:P, :])
                nc.scalar.activation(g_rstd[:], g_mv[:, :, 1], ACT.Sqrt, bias=eps[0:P, :]).then_inc(any_sqrt_done, 1)
                act.wait_ge(any_x1_ready, 1)
                with act.Fori(0, DTRIPS) as i:
                    for k in range(SLOTS):
                        act.wait_ge(any_turned1, nth(i + 1, k))
                        nc.scalar.copy(g_row_x[:, k, :], x_sb[:, bass.ds(i * SLOTS + k, 1), :]).then_inc(any_rows1_ready, 1)
                    for k in range(SLOTS):
                        act.wait_ge(any_turned1, nth(i + 2, k))
                        nc.scalar.copy(g_cols[:, k, 0, 0:P], acc[:, k * BANK:k * BANK + P]).then_inc(any_cols1_ready, 1)
                    for k in range(SLOTS):
                        act.wait_ge(any_y_ready, nth(i + 1, k))
                        nc.scalar.copy(g_y_sb[:, bass.ds(i * SLOTS + k, 1), :], acc[0:P, k * BANK:k * BANK + R * F].rearrange(
                            "p (a f) -> p a f", a=1)).then_inc(any_y_kept, 1)
                feed(2, g_rel_i)
                act.wait_ge(any_sqrt_wait, 2 * TILES)
                nc.scalar.activation(g_rstd[:], g_mv[:, :, 1], ACT.Sqrt, bias=eps[0:P, :]).then_inc(any_sqrt_done, 1)

        @block.vector
        def _(dve):

            V = nc.vector
            steps = [0]

            def step(instruction):
                steps[0] += 1
                instruction.then_inc(dve_step, 1)
                dve.wait_ge(dve_step, steps[0])

            dve.wait_ge(DST_IN, 16)
            step(V.memset(before_lim, 0.0))
            for t in range(SIGNS, TILES):
                step(V.tensor_scalar(below, dst_all, float(t * P), None, ALU.is_lt, ALU.add,
                                     accum_out=before_lim[:, t:t + 1]))
            dve.wait_ge(signs_summed, SIGNS - 1)
            step(V.tensor_scalar(before_lim[:, 1:SIGNS], sign_sums[:, 1:SIGNS], -0.5, CHUNKS / 2, ALU.mult, ALU.add))
            V.memset(rank, 0.0).then_inc(starts_counted, 1)
            dve.wait_ge(starts_summed, 1)
            V.tensor_scalar(start_i[:], ps[0:1, 7 * BANK:7 * BANK + TILES], float(E - WINDOW), None,
                            ALU.min).then_inc(starts_ready, 1)
            dve.wait_ge(high_ready, 1)
            xl = x_low.rearrange("p (t f) -> p t f", f=F)
            step(V.tensor_tensor(xl, x_sb[:], xhl[:, :, 0:F], ALU.subtract))
            V.tensor_scalar(xhl[:, :, F:2 * F], xl, LOW, None, ALU.mult).then_inc(pairs_ready, 1)

            def count_outside(c, checks, limit):
                n, width = checks.shape
                step(V.tensor_scalar(is_out[0:n, 0:width], checks, limit, None, ALU.is_gt, ALU.add,
                                     accum_out=outside[0:n, 2 * c:2 * c + 1]))
                step(V.tensor_scalar(is_out[0:n, 0:width], checks, -limit, None, ALU.is_lt, ALU.add,
                                     accum_out=outside[0:n, 2 * c + 1:2 * c + 2]))

            dve.wait_ge(pairs_ready, 1)
            step(V.memset(outside, 0.0))
            count_outside(0, x_sb[:].rearrange("p t f -> p (t f)"), X_LIMIT)

            for queue, tiles in enumerate(np.diff((0, *WINDOW_SHARES, TILES)).tolist()):
                dve.wait_ge(WIN_IN[queue], 16 * tiles)
            dve.wait_ge(consts, 2)
            V.tensor_copy(src_n, win[:, 0, :])
            V.tensor_copy(typ_n, win[:, 2, :])
            step(V.tensor_copy(dst_lo, win[:, 1, :]))
            step(V.tensor_copy(src_lo, win[:, 3, :]))
            step(V.tensor_tensor(src_lo, src_lo, dst_lo, ALU.not_equal))
            step(V.tensor_tensor(is_self, src_n, dst_lo, ALU.is_equal))
            step(V.tensor_tensor(is_self, is_self, src_lo, ALU.mult))
            for node, hi in ((src_n, src_hi), (dst_lo, dst_hi)):
                step(V.tensor_scalar(hi, node, 0.5, 1.0 / P, ALU.add, ALU.mult))
                step(V.tensor_scalar(hi, hi, -0.5, ROUND, ALU.add, ALU.add))
                step(V.tensor_scalar(hi, hi, ROUND, None, ALU.subtract))
            V.scalar_tensor_tensor(out=src_lo, in0=src_hi, scalar=-float(P), in1=src_n, op0=ALU.mult, op1=ALU.add)
            V.tensor_tensor(is_in, dst_hi, tile_of, ALU.is_equal)
            step(V.scalar_tensor_tensor(out=dst_lo, in0=dst_hi, scalar=-float(P), in1=dst_lo, op0=ALU.mult, op1=ALU.add))
            step(V.tensor_scalar(dst_n, src_hi, -1.0, float(TILES), ALU.mult, ALU.add))
            step(V.tensor_tensor(dst_n, dst_n, is_self, ALU.mult))
            step(V.tensor_tensor(dst_n, dst_n, src_hi, ALU.add))
            step(V.scalar_tensor_tensor(out=bucket_of, in0=dst_n, scalar=1.0, in1=is_in, op0=ALU.add, op1=ALU.mult))
            for b in range(KEYS):
                mark = V.tensor_scalar(bucket[:, b, :], bucket_of, float(b + 1), None, ALU.is_equal)
            mark.then_inc(buckets_marked, 1)
            dve.wait_ge(W_IN, 16 * 9)
            checked = ((w1s[:], WEIGHT_LIMIT), (w1n[:], WEIGHT_LIMIT),
                       (w2[:], WEIGHT_LIMIT), (w2t[:], WEIGHT_LIMIT), (b1a[:], BIAS_LIMIT), (b1b[:], BIAS_LIMIT))
            for c, (checks, limit) in enumerate(checked):
                count_outside(c + 1, checks, limit)
            marks = bucket.rearrange("p b (t j) -> p (b t) j", j=J)
            ahead = before.rearrange("p b (t j) -> p (b t) j", j=J)
            dve.wait_ge(prefixes_counted, 1)
            for h in range(2):
                step(V.tensor_copy(ahead[:, h * HALF:(h + 1) * HALF, 0:1],
                                   ps[0:ROWS, (2 + h) * BANK:(2 + h) * BANK + HALF].rearrange("p (c a) -> p c a", a=1)))
            for j in range(1, J):
                step(V.tensor_tensor(ahead[:, :, j], ahead[:, :, j - 1], marks[:, :, j - 1], ALU.add))
            V.tensor_tensor(before, before, bucket, ALU.mult).then_inc(ranks_parts, 1)
            dve.wait_ge(WINW_IN, 16 * TILES)
            count_outside(len(checked) + 1, win_w.rearrange("p t j -> p (t j)"), EDGE_LIMIT)
            V.tensor_copy(outside_h, outside).then_inc(limits_checked, 1)
            dve.wait_ge(WINW_IN, 16 * TILES)
            V.scalar_tensor_tensor(out=rel_row, in0=typ_n, scalar=float(N), in1=src_n, op0=ALU.mult, op1=ALU.add)
            V.tensor_scalar(is_r1, typ_n, 1.0, None, ALU.is_equal)
            step(V.scalar_tensor_tensor(out=dst_lo, in0=dst_lo, scalar=1.0, in1=is_in, op0=ALU.add, op1=ALU.mult))
            step(V.tensor_scalar(src_n, win_w.rearrange("p t j -> p (t j)"), 1.0, 0.5, ALU.add, ALU.mult))
            V.tensor_tensor(src_n, src_n, is_r1, ALU.mult).then_inc(dve_step, 1)
            steps[0] += 1
            step(V.tensor_scalar(is_r1, is_r1, -1.0, 1.0, ALU.mult, ALU.add))
            V.tensor_tensor(src_n, src_n, is_r1, ALU.add).then_inc(numbers_ready, 1)
            dve.wait_ge(numbers_ready, 1)
            V.tensor_scalar(values[:, 0, :], src_lo, 1.0, None, ALU.add)
            V.scalar_tensor_tensor(out=values[:, 1, :], in0=typ_n, scalar=float(TYPE_STEP), in1=dst_lo,
                                   op0=ALU.mult, op1=ALU.add)
            step(V.tensor_scalar(values[:, 2, :], src_n, WEIGHT_SCALE, None, ALU.mult))
            step(V.scalar_tensor_tensor(out=values[:, 3, :], in0=src_n, scalar=WEIGHT_SCALE, in1=values[:, 2, :],
                                        op0=ALU.mult, op1=ALU.subtract))
            dve.wait_ge(buckets_counted, 1)
            step(V.tensor_copy(flag_row, ps[0:1, 0:2 * BANK].rearrange("p (b c) -> p b c", b=2)[:, :, 0:HALF]))
            dve.wait_ge(limits_summed, 1)
            step(V.tensor_reduce(flag_f[0:1, 4:5], ps[0:1, 4 * BANK:4 * BANK + 16], AX.X, ALU.add))
            V.tensor_scalar(flag_f[0:1, 4:5], flag_f[0:1, 4:5], 0.5, None, ALU.is_lt)
            V.tensor_reduce(flag_f[0:1, 0:1], flag_row, AX.XY, ALU.max)
            step(V.tensor_reduce(flag_f[0:1, 1:2], flag_row, AX.XY, ALU.add))
            V.tensor_scalar(flag_f[0:1, 2:3], flag_f[0:1, 0:1], float(RANKS), None, ALU.is_le)
            step(V.tensor_scalar(flag_f[0:1, 3:4], flag_f[0:1, 1:2], float(E), None, ALU.is_equal))
            step(V.tensor_tensor(flag_f[0:1, 3:4], flag_f[0:1, 3:4], flag_f[0:1, 4:5], ALU.mult))
            V.tensor_tensor(flag_i[:], flag_f[0:1, 2:3], flag_f[0:1, 3:4], ALU.mult).then_inc(flag_ready, 1)

            dve.wait_ge(flag_ready, 1)
            fits = dve.value_load(flag_i[0:1, 0:1], min_val=0, max_val=1)
            with dve.If(fits):

                for k in range(SLOTS):
                    dve.sem_inc(bank_free, 1)
                dve.wait_ge(ranks_summed, 1)
                step(V.tensor_copy(rank[:, :, 0:J], ps[0:ROWS, 7 * BANK:7 * BANK + COLS].rearrange("p (t j) -> p t j", j=J)))
                dve.wait_ge(ident_made, 2)
                with dve.Fori(0, DTRIPS) as i:
                    for k in range(SLOTS):
                        dve.wait_ge(sorted_out, nth(i + 1, k))
                        V.tensor_tensor(rank_hot[:, k, :].rearrange("p (r j) -> p r j", j=JP), rank_iota,
                                        rank[:, one(i * SLOTS + k), :].broadcast_to([ROWS, RANKS, JP]),
                                        ALU.is_equal)
                        here = bass.ds((i * SLOTS + k) * J, J)
                        V.tensor_tensor(
                            record[:, k, :].rearrange("p (f b j) -> p f b j", b=KEYS, j=JP)[:, :, :, 0:J],
                            bucket[:, :, here].rearrange("p (a b) j -> p a b j", a=1).broadcast_to([ROWS, FIELDS, KEYS, J]),
                            values[:, :, here].rearrange("p f (a j) -> p f a j", a=1).broadcast_to([ROWS, FIELDS, KEYS, J]),
                            ALU.mult).then_inc(rank_hot_ready, 1)
                dve.wait_ge(ident_made, 4)
                dve.wait_ge(pairs_ready, 1)
                dve.wait_ge(sorted_kept, nth(DTRIPS + 1, SLOTS - 1))
                def tile_hot(t, h, f):
                    w, at = SPLIT[h], f * KEYS + h * SPLIT[0]
                    return V.tensor_tensor(
                        (src_hot, dst_hot)[f][h].rearrange("p (n b) -> p n b", b=w), place_iota[h],
                        buckets[:, one(t), at:at + w].broadcast_to([RANKS, P, w]), ALU.is_equal)

                for h in range(2):
                    tile_hot(0, h, 0)
                dve.wait_ge(slots_saved, 32)
                dst_place = buckets[:, :, KEYS:2 * KEYS]
                for r in range(2):
                    step(V.tensor_scalar(type_part, dst_place, TYPE_STEP + 0.5, -float(TYPE_STEP), ALU.is_gt, ALU.mult))
                    step(V.tensor_tensor(dst_place, dst_place, type_part, ALU.add))
                for h in range(2):
                    tile_hot(0, h, 1).then_inc(hots_ready[h], 1)
                with dve.Fori(1, TILES) as t:
                    for h in range(2):
                        dve.wait_ge((first_used, self_ready)[h], t + 1)
                        w, at = SPLIT[h], h * SPLIT[0]
                        V.tensor_tensor(
                            both_hot[h].rearrange("p f (n b) -> p f n b", b=w),
                            place_iota[h].rearrange("p (a n) b -> p a n b", a=1).broadcast_to([RANKS, 2, P, w]),
                            buckets[:, one(t), 0:2 * KEYS].rearrange("p a (f b) -> p f a b", b=KEYS)[
                                :, :, :, at:at + w].broadcast_to([RANKS, 2, P, w]), ALU.is_equal).then_inc(hots_ready[h], 1)

                def mean(t, k):
                    s = t * 4
                    dve.wait_ge(sums_ready, t + 1)
                    V.tensor_scalar(rstd[:, k:k + 1], conv_bank(k, 2 * F, 2 * F + 1)[0:P, :],
                                    self_count[:, one(t)], 1.0, ALU.add, ALU.max).then_inc(conv_step, 1)
                    dve.wait_ge(conv_step, s + 1)
                    V.reciprocal(rstd[:, k:k + 1], rstd[:, k:k + 1]).then_inc(conv_step, 1)
                    dve.wait_ge(conv_step, s + 2)
                    V.tensor_copy(deg_inv[:, one(t)], rstd[:, k:k + 1])
                    V.tensor_tensor(self_inv[:, one(t)], self_count[:, one(t)], rstd[:, k:k + 1], ALU.mult)
                    V.tensor_scalar(low[:, k % 2, :], conv_bank(k, F, 2 * F)[0:P, :], rstd[:, k:k + 1],
                                    1.0 / LOW, ALU.mult, ALU.mult).then_inc(conv_step, 1)
                    dve.wait_ge(conv_step, s + 3)
                    V.scalar_tensor_tensor(out=low[:, k % 2, :], in0=conv_bank(k, 0, F)[0:P, :],
                                           scalar=rstd[:, k:k + 1], in1=low[:, k % 2, :],
                                           op0=ALU.mult, op1=ALU.add).then_inc(conv_step, 1)
                    dve.wait_ge(conv_step, s + 4)
                    dve.wait_ge(g_ready, t + 1)
                    V.scalar_tensor_tensor(out=row_m[0:P, k, :], in0=x_sb[:, one(t), :].rearrange("p a f -> p (a f)"),
                                           scalar=self_inv[:, one(t)], in1=low[:, k % 2, :],
                                           op0=ALU.mult, op1=ALU.add).then_inc(mean_ready, 1)

                def self_part(t, k):
                    s = t * 2
                    xt = x_sb[:, one(t), :].rearrange("p a f -> p (a f)")
                    g = conv_bank(k, 0, F)[0:P, :]
                    dve.wait_ge(g_high, t + 1)
                    V.tensor_tensor(xt, conv_bank(k, F, 2 * F)[0:P, :], xt, ALU.add).then_inc(self_step, 1)
                    dve.wait_ge(self_step, s + 1)
                    V.tensor_tensor(xt, xt, b2r[:], ALU.add).then_inc(self_step, 1)
                    dve.wait_ge(self_step, s + 2)
                    V.scalar_tensor_tensor(out=xt, in0=g, scalar=self_inv[:, one(t)], in1=xt, op0=ALU.mult, op1=ALU.add)
                    V.tensor_tensor(low[:, k % 2, :], g,
                                    ghl[:, one(t), 0:F].rearrange("p a f -> p (a f)"), ALU.subtract).then_inc(bank_free, 1)
                    dve.wait_ge(bank_free, t + (SLOTS + 1))
                    V.tensor_scalar(ghl[:, one(t), F:2 * F], low[:, k % 2:k % 2 + 1, :], LOW, None,
                                    ALU.mult).then_inc(g_pairs, 1)

                def first_conv(back, has):
                    if has(1):
                        mean(*back(1)[0:2])
                    if has(4):
                        self_part(*back(4)[0:2])

                dve.wait_ge(self_kept, TILES + 1)
                pipeline(dve, first_conv)

                dve.wait_ge(g_pairs, TILES)

                def second_conv(back, has):
                    if has(0):
                        t, k, _ = back(0)
                        s = t * 4
                        xt = x_sb[:, one(t), :].rearrange("p a f -> p (a f)")
                        dve.wait_ge(sums2_ready, t + 1)
                        if has(4):
                            dve.wait_ge(x1_pairs, t - 3)
                        V.tensor_scalar(low[:, k % 2, :], conv_bank(k, F, 2 * F)[0:P, :], deg_inv[:, one(t)],
                                        1.0 / LOW, ALU.mult, ALU.mult).then_inc(conv2_step, 1)
                        dve.wait_ge(conv2_step, s + 1)
                        V.scalar_tensor_tensor(out=low[:, k % 2, :], in0=conv_bank(k, 0, F)[0:P, :],
                                               scalar=deg_inv[:, one(t)], in1=low[:, k % 2, :],
                                               op0=ALU.mult, op1=ALU.add).then_inc(conv2_step, 1)
                        dve.wait_ge(conv2_step, s + 2)
                        V.tensor_tensor(row_m[0:P, k, :], low[:, k % 2, :], xt, ALU.add).then_inc(conv2_step, 1)
                        dve.wait_ge(conv2_step, s + 3)
                        V.bn_stats(stats[:, k, :], row_m[0:P, k, :]).then_inc(conv2_step, 1)
                        dve.wait_ge(conv2_step, s + 4)
                        dve.sem_inc(wait_taken, 1)
                        V.bn_aggr(mv[:, k, :], stats[:, k, :]).then_inc(var2_ready, 1)
                    if has(1):
                        t, k, _ = back(1)
                        dve.wait_ge(root2_ready, t + 1)
                        V.reciprocal(rstd[:, k:k + 1], rstd[:, k:k + 1]).then_inc(root_inv, 1)
                        dve.wait_ge(root_inv, t + 1)
                        dve.wait_ge(y_ready, t + 1)
                        V.tensor_scalar(row_x[0:P, k, :], row_m[0:P, k, :], mv[:, k, 0:1], rstd[:, k:k + 1],
                                        ALU.subtract, ALU.mult).then_inc(x1_ready, 1)
                    if has(3):
                        t, k, _ = back(3)
                        dve.wait_ge(x1_kept, t + 1)
                        V.tensor_tensor(low[:, k % 2:k % 2 + 1, :], x_sb[:, one(t), :], x1hl[:, one(t), 0:F],
                                        ALU.subtract).then_inc(low_step, 1)
                        dve.wait_ge(low_step, t + 1)
                        V.tensor_scalar(x1hl[:, one(t), F:2 * F], low[:, k % 2:k % 2 + 1, :], LOW, None,
                                        ALU.mult).then_inc(x1_pairs, 1)

                pipeline(dve, second_conv)
                dve.wait_ge(L1_IN, 16 * 3)
                dst_typ = records[:, :, KEYS:2 * KEYS]
                for r in (1, 2):
                    step(V.tensor_scalar(place_typ[r], dst_typ, -float(r * TYPE_STEP), None, ALU.add))

                def one_hots(q, h, fresh=False):
                    w, at = SPLIT[h], h * SPLIT[0]
                    if not fresh:
                        dve.wait_ge(block_built, q * KEYS + (at + w - KEYS))
                    t = one(q * 2 + 1)
                    hot = lambda v: hots[h][:, v, :].rearrange("p (n b) -> p n b", b=w)
                    col = lambda f: records[:, t, f * KEYS + at:f * KEYS + at + w].broadcast_to([RANKS, P, w])
                    typ = lambda r: place_typ[r][:, t, at:at + w].broadcast_to([RANKS, P, w])
                    V.tensor_tensor(hot(4), places[h], typ(1), ALU.is_equal).then_inc(hot1_step, 1)
                    V.tensor_tensor(hot(0), places[h], col(0), ALU.is_equal)
                    V.tensor_tensor(hot(1), places[h], col(1), ALU.is_equal)
                    V.tensor_tensor(hot(2), places[h], typ(2), ALU.is_equal)
                    dve.wait_ge(hot1_step, q * 4 + (2 * h + 1))
                    V.tensor_tensor(hot(3), hot(4), col(2), ALU.mult).then_inc(hot1_step, 1)
                    dve.wait_ge(hot1_step, q * 4 + (2 * h + 2))
                    V.tensor_tensor(hot(4), hot(4), col(3), ALU.mult).then_inc(hots_made[h], 1)

                def destinations(q, u, fresh=False):
                    if not fresh:
                        dve.wait_ge(tile_done, q - 1)
                    for j in range(J):
                        c = q * (2 * J) + j
                        made = V.tensor_scalar(dst_t[:, u, j * P:(j + 1) * P], place_f, scales_in[:, one(c)],
                                               scales_in[:, one(c + COLS)], ALU.is_equal, ALU.mult)
                    made.then_inc(dst_ready, 1)

                one_hots(0, 0, True)
                dve.wait_ge(place_made, 1)
                one_hots(0, 1, True)
                destinations(0, 0, True)
                dve.wait_ge(bn_root, 1)
                step(V.reciprocal(bn_s, bn_s))
                step(V.tensor_tensor(bn_a, bn_s, bn[:, 0, :], ALU.mult))
                step(V.tensor_tensor(bn_b, bn_a, bn[:, 2, :], ALU.mult))
                step(V.tensor_tensor(bn_b, bn[:, 1, :], bn_b, ALU.subtract))

                def join_sums(q):
                    dve.wait_ge(sums_copied, q + 1)
                    V.scalar_tensor_tensor(out=dense_sums[:, 0:2, :].rearrange("p a n -> p (a n)"),
                                           in0=ps[:, LOWER:LOWER + 2 * P],
                                           scalar=1.0 / LOW, in1=sum_high, op0=ALU.mult, op1=ALU.add).then_inc(sums_joined, 1)

                def norm_in(q, kind):
                    s = q * 8 + 4 * (1 - kind)
                    t = q * 2 + (1 - kind)
                    xt = x_sb[:, one(t), :].rearrange("p a f -> p (a f)")
                    z = z_t[:, kind, :]
                    dve.wait_ge((dense_done, tile_done)[kind], q + 1)
                    read = (dense_read, acc_read)[kind]
                    o = (DENSE, GATHERED)[kind]
                    V.tensor_tensor(z, ps[0:P, o:o + F], xt, ALU.add).then_inc(read, 1)
                    dve.wait_ge(read, q + 1)
                    V.tensor_tensor(z, z, bn_a, ALU.mult).then_inc(norm_step, 1)
                    dve.wait_ge(norm_step, s + 1)
                    V.tensor_tensor(z, z, bn_b, ALU.add).then_inc(norm_step, 1)
                    dve.wait_ge(norm_step, s + 2)
                    V.scalar_tensor_tensor(out=z, in0=z, scalar=0.0, in1=xt, op0=ALU.max, op1=ALU.add).then_inc(norm_step, 1)
                    dve.wait_ge(norm_step, s + 3)
                    V.bn_stats(stats[:, kind, :], z).then_inc(norm_step, 1)
                    dve.wait_ge(norm_step, s + 4)
                    dve.sem_inc(wait_taken, 1)
                    V.bn_aggr(mv[:, kind, :], stats[:, kind, :]).then_inc(var3_ready, 1)

                def norm_out(q, kinds=(0, 1)):
                    dve.wait_ge(root3_ready, q + 1)
                    V.reciprocal(rstd[:, kinds[0]:2], rstd[:, kinds[0]:2]).then_inc(root_inv3, 1)
                    dve.wait_ge(root_inv3, q + 1)
                    for kind in kinds:
                        V.tensor_scalar(result[:, one(q * 2 + (1 - kind)), :].rearrange("p a f -> p (a f)"), z_t[:, kind, :],
                                        mv[:, kind, 0:1], rstd[:, kind:kind + 1],
                                        ALU.subtract, ALU.mult).then_inc(out_ready, 1)

                def pair(q, u, last=False):
                    join_sums(q - 1)
                    norm_in(q - 1, 1)
                    one_hots(q, 1)
                    norm_in(q - 1, 0)
                    destinations(q, u, isinstance(q, int) and q < 2)
                    norm_out(q - 1)
                    if not last:
                        one_hots(q + 1, 0)

                one_hots(1, 0)
                pair(1, 1)
                with dve.Fori(1, PAIRS // 2 - 1) as i:
                    for u in range(2):
                        pair(i * 2 + u, u)
                pair(PAIRS - 2, 0)
                pair(PAIRS - 1, 1, last=True)
                destinations(PAIRS, 0)
                join_sums(PAIRS - 1)
                dve.wait_ge(out_ready, 2 * PAIRS - 2)
                norm_in(PAIRS - 1, 1)
                norm_in(PAIRS - 1, 0)
                norm_out(PAIRS - 1)
                dve.wait_ge(out_ready, 2 * PAIRS)
                norm_in(PAIRS, 1)
                norm_out(PAIRS, (1,))

            with dve.Else():
                dve.wait_ge(WINW_IN, 16 * TILES)
                steps = [0]

                def step(instruction):
                    steps[0] += 1
                    instruction.then_inc(any_dve_step, 1)
                    dve.wait_ge(any_dve_step, steps[0])

                flat = "p t f -> p (t f)"
                for k in range(SLOTS):
                    dve.sem_inc(any_g_kept, 1)
                dve.wait_ge(EDGES_IN, 32)
                dve.wait_ge(any_const_made, 1)
                step(V.tensor_copy(g_dst_f[:], g_dst_i[:]))
                step(V.tensor_scalar(g_dst_hi[:], g_dst_f[:], 0.5, 1.0 / P, ALU.add, ALU.mult))
                step(V.tensor_scalar(g_dst_hi[:], g_dst_hi[:], -0.5, ROUND, ALU.add, ALU.add))
                step(V.tensor_scalar(g_dst_hi[:], g_dst_hi[:], ROUND, None, ALU.subtract))
                step(V.scalar_tensor_tensor(out=g_dst_lo[:], in0=g_dst_hi[:], scalar=-float(P), in1=g_dst_f[:],
                                            op0=ALU.mult, op1=ALU.add))
                with dve.Fori(0, TRIPS) as i:
                    for k in range(SLOTS):
                        c = bass.ds(i * SLOTS + k, 1)
                        dve.wait_ge(any_deg_used, nth(i + 1, k))
                        V.tensor_scalar(g_lo_hot[:, k, :], g_node_iota[:, 0:P], g_dst_lo[:, c], None, ALU.is_equal)
                        V.tensor_scalar(g_hi_hot[:, k, :], g_node_iota[:, 0:TILES], g_dst_hi[:, c], None,
                                        ALU.is_equal).then_inc(any_deg_hot, 1)
                dve.wait_ge(TYPES_IN, 32)
                V.tensor_copy(g_src_f[:], g_src_i[:])
                step(V.tensor_copy(g_typ_f[:], g_typ_i[:]))
                V.scalar_tensor_tensor(out=g_rel_i[:], in0=g_typ_f[:], scalar=float(N), in1=g_src_f[:],
                                       op0=ALU.mult, op1=ALU.add)
                V.tensor_scalar(g_is_r1[:], g_typ_f[:], 1.0, None, ALU.is_equal)
                step(V.tensor_scalar(g_scale[:], g_w_sb[:], 1.0, 0.5, ALU.add, ALU.mult))
                step(V.scalar_tensor_tensor(out=g_scale[:], in0=g_scale[:], scalar=0.0, in1=g_is_r1[:], op0=ALU.add, op1=ALU.mult))
                step(V.tensor_scalar(g_is_r1[:], g_is_r1[:], -1.0, 1.0, ALU.mult, ALU.add))
                step(V.tensor_tensor(g_scale[:], g_scale[:], g_is_r1[:], ALU.add))
                dve.wait_ge(any_deg_ready, 1)
                V.tensor_copy(g_deg[:], acc[0:P, DEG:DEG + TILES])
                step(V.tensor_scalar(deg_inv[:], acc[0:P, DEG:DEG + TILES], 1.0, None, ALU.max))
                step(V.reciprocal(deg_inv[:], deg_inv[:]))
                step(V.tensor_scalar(g_deg[:], g_deg[:], 0.0, None, ALU.is_gt))
                V.tensor_tensor(deg_inv[:], deg_inv[:], g_deg[:], ALU.mult).then_inc(any_deg_kept, 1)
                dve.wait_ge(any_deg_kept, 1)

                def onehots(layer):
                    with dve.Fori(0, TRIPS) as i:
                        for k in range(SLOTS):
                            c = bass.ds(i * SLOTS + k, 1)
                            dve.wait_ge(any_chunk_done, nth(i + 1 + TRIPS * layer, k))
                            if layer == 2:
                                V.tensor_scalar(g_onehot[:, k, :], g_node_iota[:], g_dst_f[:, c], g_scale[:, c], ALU.is_equal,
                                                ALU.mult).then_inc(any_onehot_ready, 1)
                            else:
                                V.tensor_scalar(g_onehot[:, k, :], g_node_iota[:], g_dst_f[:, c], None,
                                                ALU.is_equal).then_inc(any_onehot_ready, 1)

                def summed(layer):
                    dve.wait_ge(any_chunk_done, nth(TRIPS * (layer + 1) + 1, SLOTS - 1))

                sums = acc[0:P, 0:ACC].rearrange("p (t f) -> p t f", f=F)
                inv_bc = deg_inv[:].rearrange("p (t a) -> p t a", a=1).broadcast_to([P, TILES, F])

                def layer_norm(rows, n):
                    with dve.Fori(0, TILES) as t:
                        V.bn_stats(g_stats[:, bass.ds(t, 1), :], rows[:, bass.ds(t, 1), :]).then_inc(any_stats_made, 1)
                    dve.wait_ge(any_stats_made, n * TILES)
                    for t in range(TILES):
                        V.bn_aggr(g_mv[:, t, :], g_stats[:, t, :]).then_inc(any_sqrt_wait, 1)
                    dve.wait_ge(any_sqrt_done, n)
                    step(V.reciprocal(g_rstd[:], g_rstd[:]))
                    mean = g_mv[:, :, 0:1].broadcast_to([P, TILES, F])
                    step(V.tensor_tensor(rows[:], rows[:], mean, ALU.subtract))
                    r = g_rstd[:].rearrange("p (t a) -> p t a", a=1).broadcast_to([P, TILES, F])
                    V.tensor_tensor(x_sb[:], rows[:], r, ALU.mult).then_inc(any_normed, 1)
                    dve.wait_ge(any_normed, n)

                onehots(0)
                summed(0)
                V.tensor_tensor(g_mean_sb[:], sums, inv_bc, ALU.mult).then_inc(any_mean_ready, 1)
                dve.wait_ge(X_IN, 16)
                dve.wait_ge(W_IN, 16 * 9)
                b2_bc = b2r[:].rearrange("p (a f) -> p a f", a=1).broadcast_to([P, TILES, F])
                step(V.tensor_tensor(g_self_sb[:], x_sb[:], b2_bc, ALU.add))
                with dve.Fori(0, DTRIPS) as i:
                    for k in range(SLOTS):
                        dve.wait_ge(any_g_ready, nth(i + 1, k))
                        t = bass.ds(i * SLOTS + k, 1)
                        V.tensor_tensor(g_self_sb[:, t, :], g_self_sb[:, t, :],
                                        acc[0:P, k * BANK + F:k * BANK + 2 * F].rearrange("p (a f) -> p a f", a=1), ALU.add)
                        V.tensor_copy(g_g_sb[:, t, :], acc[0:P, k * BANK:k * BANK + F].rearrange("p (a f) -> p a f", a=1)).then_inc(any_g_kept, 1)
                onehots(1)
                summed(1)
                step(V.tensor_tensor(g_mean_sb[:], sums, inv_bc, ALU.mult))
                step(V.tensor_tensor(g_mean_sb[:], g_mean_sb[:], g_self_sb[:], ALU.add))
                dve.wait_ge(any_BN_IN, 64)
                layer_norm(g_mean_sb, 1)
                step(V.reciprocal(g_bn_s[:], g_bn_s[:]))
                step(V.tensor_tensor(g_bn_a[:], g_bn_s[:], g_bn[:, 0, :], ALU.mult))
                step(V.tensor_tensor(g_bn_b[:], g_bn_a[:], g_bn[:, 2, :], ALU.mult))
                V.tensor_tensor(g_bn_b[:], g_bn[:, 1, :], g_bn_b[:], ALU.subtract).then_inc(any_x1_ready, 1)
                dve.wait_ge(any_x1_ready, 1)
                for k in range(SLOTS):
                    dve.wait_ge(any_y_stored[k], 16 * DTRIPS)
                onehots(2)
                summed(2)
                step(V.tensor_tensor(g_mean_sb[:], sums, x_sb[:], ALU.add))
                bc = lambda v: v[:].rearrange("p (a f) -> p a f", a=1).broadcast_to([P, TILES, F])
                step(V.tensor_tensor(g_mean_sb[:], g_mean_sb[:], bc(g_bn_a), ALU.mult))
                step(V.tensor_tensor(g_mean_sb[:], g_mean_sb[:], bc(g_bn_b), ALU.add))
                step(V.scalar_tensor_tensor(out=g_mean_sb[:].rearrange(flat), in0=g_mean_sb[:].rearrange(flat), scalar=0.0,
                                            in1=x_sb[:].rearrange(flat), op0=ALU.max, op1=ALU.add))
                layer_norm(g_mean_sb, 2)

        @block.tensor
        def _(pe):

            mm = nc.tensor.matmul
            pe.wait_ge(starts_counted, 1)
            pe.wait_ge(consts, 1)
            mm(ps[0:1, 7 * BANK:7 * BANK + TILES], ones_f, before_lim, start=True, stop=True).then_inc(starts_summed, 1)
            pe.wait_ge(buckets_marked, 1)
            pe.wait_ge(ident_made, 1)
            marks = bucket.rearrange("p b (t j) -> p (b t) j", j=J)
            for h in range(2):
                for j in range(J):
                    last = mm(ps[0:ROWS, (2 + h) * BANK:(2 + h) * BANK + HALF], lower, marks[:, h * HALF:(h + 1) * HALF, j],
                              start=(j == 0), stop=(j == J - 1))
            last.then_inc(prefixes_counted, 1)
            for h in range(2):
                for j in range(J):
                    last = mm(ps[0:1, h * BANK:h * BANK + HALF], ones_h[:, 0:1], marks[:, h * HALF:(h + 1) * HALF, j],
                              start=(j == 0), stop=(j == J - 1))
            last.then_inc(buckets_counted, 1)
            pe.wait_ge(ranks_parts, 1)
            for b in range(KEYS):
                last = mm(ps[0:ROWS, 7 * BANK:7 * BANK + COLS], ident_h, before[:, b, :], start=(b == 0), stop=(b == KEYS - 1))
            last.then_inc(ranks_summed, 1)
            pe.wait_ge(limits_checked, 1)
            mm(ps[0:1, 4 * BANK:4 * BANK + 16], ones_all, outside_h, start=True, stop=True).then_inc(limits_summed, 1)

            pe.wait_ge(flag_ready, 1)
            fits = pe.value_load(flag_i[0:1, 0:1], min_val=0, max_val=1)
            with pe.If(fits):

                for k in range(SLOTS):
                    for credit in (sorted_out, g_ready, y_ready):
                        pe.sem_inc(credit, 1)
                pe.sem_inc(first_used, 1)
                pe.sem_inc(self_ready, 1)
                with pe.Fori(0, DTRIPS) as i:
                    for k in range(SLOTS):
                        pe.wait_ge(rank_hot_ready, nth(i + 1, k))
                        pe.wait_ge(sorted_kept, nth(i + 1, k))
                        hot = rank_hot[:, k, :].rearrange("p (r j) -> p r j", j=JP)
                        fields = record[:, k, :].rearrange("p (g j) -> p g j", j=JP)
                        for j in range(J):
                            last = mm(bank(k, 0, FIELDS * KEYS), hot[:, :, j], fields[:, :, j],
                                      start=(j == 0), stop=(j == J - 1))
                        last.then_inc(sorted_out, 1)
                pe.wait_ge(sorted_kept, nth(DTRIPS + 1, SLOTS - 1))
                with pe.Fori(0, TILES) as t:
                    for h, w in enumerate(SPLIT):
                        pe.wait_ge(hots_ready[h], t + 1)
                        s_hot = src_hot[h].rearrange("p (n b) -> p n b", b=w)
                        d_hot = dst_hot[h].rearrange("p (n b) -> p n b", b=w)
                        for b in range(w):
                            key = h * SPLIT[0] + b
                            g, n = divmod(key, 4)
                            if key == TILES:
                                pe.wait_ge(self_kept, t + 1)
                                mm(ps[0:P, 7 * BANK:7 * BANK + 1], d_hot[:, :, b], ones_r[:],
                                   start=True, stop=True).then_inc(self_ready, 1)
                                break
                            if n == 0:
                                pe.wait_ge(blocks_kept, t * GROUPS + g + 1)
                            last = mm(ps[0:P, g * BANK + n * P:g * BANK + (n + 1) * P], s_hot[:, :, b], d_hot[:, :, b],
                                      start=True, stop=True)
                            if n == 3 or key == TILES - 1:
                                last.then_inc(blocks_ready, 1)
                            if key == SPLIT[0] - 1:
                                last.then_inc(first_used, 1)
                pe.wait_ge(blocks_kept, TILES * GROUPS + GROUPS)
                pe.wait_ge(self_kept, TILES + 1)

                def first_conv(back, has):
                    if has(0):
                        t, k, _ = back(0)
                        pe.wait_ge(bank_free, t + 1)
                        for b in range(TILES):
                            last = mm(conv_bank(k, 0, 2 * F + 1)[0:P, :],
                                      adj[:, one(t), b * P:(b + 1) * P].rearrange("p a n -> p (a n)"),
                                      xhl[:, b, 0:2 * F + 1], start=(b == 0), stop=(b == TILES - 1))
                        last.then_inc(sums_ready, 1)
                    if has(1):
                        t, k, _ = back(1)
                        pe.wait_ge(row_ready, t + 1)
                        pe.wait_ge(mean_ready, t + 1)
                        nc.tensor.transpose(conv_bank(k, 0, P), row_x[0:P, k, :], ident[0:P, 0:P])
                        nc.tensor.transpose(conv_bank(k, 128, 128 + P), row_m[0:P, k, :], ident[0:P, 0:P]).then_inc(turned, 1)
                    if has(2):
                        t, k, _ = back(2)
                        pe.wait_ge(cols_ready, t + 1)
                        xT, mT = cols[:, k, 0:P], cols[:, k, 128:128 + P]
                        h, tail = conv_bank(k, 256, 256 + P), conv_bank(k, 384, 384 + P)[0:H2, :]
                        mm(h, w1s[:, 0:F], xT, start=True, stop=False)
                        mm(h, w1n[:, 0:F], mT, start=False, stop=True)
                        mm(tail, w1s[:, F:H], xT, start=True, stop=False)
                        mm(tail, w1n[:, F:H], mT, start=False, stop=True).then_inc(h_ready, 1)
                    if has(3):
                        t, k, _ = back(3)
                        pe.wait_ge(relu_done, t + 1)
                        g = conv_bank(k, 0, 2 * F)[0:P, :]
                        mm(g, row_m[:, k, 0:P], w2[:], start=True, stop=False)
                        mm(g, row_x[0:H2, k, 0:P], w2t[:], start=False, stop=True).then_inc(g_ready, 1)

                pe.wait_ge(pairs_ready, 1)
                pe.wait_ge(W_IN, 16 * 9)
                pipeline(pe, first_conv)
                pe.wait_ge(WR_IN, 16)
                for r in range(R):
                    nc.tensor.transpose(ps[:, 7 * BANK + r * F:7 * BANK + (r + 1) * F], wr[:, r * F:(r + 1) * F],
                                        ident[:]).then_inc(wr_turned, 1)
                pe.wait_ge(g_pairs, TILES)
                pe.wait_ge(wr_kept, 1)
                def second_conv(back, has):
                    if has(0):
                        t, k, _ = back(0)
                        pe.wait_ge(y_kept, t + 1)
                        for b in range(TILES):
                            last = mm(conv_bank(k, 0, 2 * F)[0:P, :],
                                      adj[:, one(t), b * P:(b + 1) * P].rearrange("p a n -> p (a n)"),
                                      ghl[:, b, :], start=(b == 0), stop=(b == TILES - 1))
                        last.then_inc(sums2_ready, 1)
                    if has(2):
                        t, k, _ = back(2)
                        pe.wait_ge(x1_ready, t + 1)
                        nc.tensor.transpose(conv_bank(k, 384, 384 + P), row_x[0:P, k, :], ident[0:P, 0:P]).then_inc(turned2, 1)
                    if has(3):
                        t, k, _ = back(3)
                        pe.wait_ge(cols2_ready, t + 1)
                        mm(conv_bank(k, 0, R * F)[0:P, :], cols[:, k, 0:P], wrT, start=True, stop=True).then_inc(y_ready, 1)

                pipeline(pe, second_conv)
                pe.wait_ge(y_kept, nth(DTRIPS + 1, SLOTS - 1))
                pe.wait_ge(self_kept, TILES + 1)

                def dense_out(q):
                    pe.wait_ge(sums_joined, q + 1)
                    pe.wait_ge(sums_copied, q + 1)
                    if not isinstance(q, int) or q > 0:
                        pe.wait_ge(dense_read, q)
                    for n, r in enumerate((0, 2, 1)):
                        last = mm(ps[0:P, DENSE:DENSE + F], dense_sums[:, n, :], wrT[:, r * F:(r + 1) * F],
                                  start=(n == 0), stop=(n == 2))
                    last.then_inc(dense_done, 1)

                def build(q, b, first):
                    h = int(b >= SPLIT[0])
                    hot = hots[h].rearrange("p v (n b) -> p (v n) b", b=SPLIT[h])[:, :, b - h * SPLIT[0]]
                    if b in (0, SPLIT[0]):
                        pe.wait_ge(hots_made[h], q + 1)
                    if not (first and b < BUILD_BANKS):
                        pe.wait_ge(block_kept, q * KEYS + previous_use(b, BUILD_BANKS))
                    o = b % BUILD_BANKS * BANK
                    source = hot[:, 0:P]
                    mm(ps[0:P, o:o + 2 * P], source, hot[:, P:3 * P], start=True, stop=True)
                    mm(ps[0:P, o + 2 * P:o + 3 * P], source, hot[:, 3 * P:4 * P], start=True, stop=False)
                    mm(ps[0:P, o + 2 * P:o + 3 * P], source, hot[:, 4 * P:5 * P], start=False, stop=True).then_inc(block_built, 1)

                def use(q, b, u):
                    pe.wait_ge(block_kept, q * KEYS + b + 1)
                    at = b % RING
                    first, last = b == 0, b == KEYS - 1
                    if last:
                        high, lower_part = (x1hl[:, one(q * 2 + 1), c:c + F].rearrange("p a f -> p (a f)") for c in (0, F))
                        pe.wait_ge(self_copied, q + 1)
                    else:
                        high, lower_part = (x1hl[:, b, c:c + F] for c in (0, F))
                    mm(ps[:, HIGH:HIGH + 2 * P], high, a02[:, at, :], start=first, stop=last)
                    mm(ps[:, LOWER:LOWER + 2 * P], lower_part, a02[:, at, :], start=first, stop=last)
                    mm(ps[:, FULL:FULL + P], x1_self[:, u, :] if last else x_sb[:, b, :], a1[:, at, :],
                       start=first, stop=last).then_inc(block_used, 1)

                def dense(q, u, first=False):
                    for b in range(KEYS + LAG):
                        if b < KEYS:
                            build(q, b, first)
                        if b == LAG and not first:
                            pe.wait_ge(sums_joined, q)
                            pe.wait_ge(sums_copied, q)
                        if b >= LAG:
                            use(q, b - LAG, u)
                        if b == 8 and not first:
                            dense_out(q - 1)

                def gathered(q, u, i, first=False):
                    pe.wait_ge(dst_ready, q + 1)
                    if not first:
                        pe.wait_ge(acc_read, q)
                    pe.wait_ge(landed[u], (i + 1) * (16 * J))
                    for j in range(J):
                        last = mm(ps[0:P, GATHERED:GATHERED + F], dst_t[:, u, j * P:(j + 1) * P],
                                  feat_t[:, u, j * F:(j + 1) * F], start=(j == 0), stop=(j == J - 1))
                    last.then_inc(tile_done, 1)

                pe.wait_ge(x1_pairs, TILES)
                dense(0, 0, True)
                gathered(0, 0, 0, True)
                dense(1, 1)
                gathered(1, 1, 0)
                with pe.Fori(1, PAIRS // 2) as i:
                    for u in range(2):
                        dense(i * 2 + u, u)
                        gathered(i * 2 + u, u, i)
                dense_out(PAIRS - 1)
                gathered(PAIRS, 0, PAIRS // 2)

            with pe.Else():
                mm = nc.tensor.matmul

                def clear(b, width=BANK):
                    mm(acc[0:P, b * BANK:b * BANK + width], g_zeros[:], g_node_iota[:, 0:width], start=True, stop=False,
                       skip_group_check=True)

                for k in range(SLOTS):
                    for credit in (any_chunk_done, any_deg_used, any_turned, any_turned1):
                        pe.sem_inc(credit, 1)
                pe.wait_ge(any_const_made, 2)
                clear(BANKS)
                with pe.Fori(0, TRIPS) as i:
                    for k in range(SLOTS):
                        pe.wait_ge(any_deg_hot, nth(i + 1, k))
                        mm(acc[0:P, DEG:DEG + TILES], g_lo_hot[:, k, :], g_hi_hot[:, k, :], start=False, stop=False,
                           skip_group_check=True).then_inc(any_deg_used, 1)
                pe.wait_ge(any_deg_used, nth(TRIPS + 1, SLOTS - 1))
                nc.tensor.nop().then_inc(any_deg_ready, 1)

                def aggregate(layer):
                    for b in range(BANKS):
                        clear(b)
                    with pe.Fori(layer * TRIPS, (layer + 1) * TRIPS) as i:
                        for k in range(SLOTS):
                            pe.wait_ge(any_landed[k], 16 * i + 16)
                            pe.wait_ge(any_onehot_ready, nth(i + 1, k))
                            for t in range(TILES):
                                last = mm(acc[0:P, t * F:(t + 1) * F], g_onehot[:, k, t * P:(t + 1) * P], g_feat[:, k, :],
                                          start=False, stop=False, skip_group_check=True)
                            last.then_inc(any_chunk_done, 1)

                pe.wait_ge(any_deg_kept, 1)
                aggregate(0)
                pe.wait_ge(W_IN, 16 * 9)
                pe.wait_ge(WR_IN, 16)
                for r in range(R):
                    nc.tensor.transpose(acc[:, DEG + r * F:DEG + (r + 1) * F], g_wr[:, r, :], ident[:]).then_inc(any_wr_turned, 1)
                pe.wait_ge(any_mean_ready, 1)
                with pe.Fori(0, DTRIPS) as i:
                    for k in range(SLOTS):
                        pe.wait_ge(any_rows_ready, nth(i + 1, k))
                        pe.wait_ge(any_g_kept, nth(i + 1, k))
                        nc.tensor.transpose(acc[:, k * BANK:k * BANK + P], g_row_x[:, k, :], ident[0:P, 0:P])
                        nc.tensor.transpose(acc[:, k * BANK + 128:k * BANK + 128 + P], g_row_m[:, k, :],
                                            ident[0:P, 0:P]).then_inc(any_turned, 1)
                    for k in range(SLOTS):
                        pe.wait_ge(any_cols_ready, nth(i + 1, k))
                        o = k * BANK + 256
                        mm(acc[:, o:o + P], w1s[:, 0:F], g_cols[:, k, 0, 0:P], start=True, stop=False)
                        mm(acc[:, o:o + P], w1n[:, 0:F], g_cols[:, k, 1, 0:P], start=False, stop=True)
                        mm(acc[0:H2, o + 128:o + 128 + P], w1s[:, F:H], g_cols[:, k, 0, 0:P], start=True, stop=False)
                        mm(acc[0:H2, o + 128:o + 128 + P], w1n[:, F:H], g_cols[:, k, 1, 0:P], start=False,
                           stop=True).then_inc(any_h_ready, 1)
                    for k in range(SLOTS):
                        pe.wait_ge(any_relu_done, nth(i + 1, k))
                        mm(acc[0:P, k * BANK:k * BANK + 2 * F], any_hT[:, k, :], w2[:], start=True, stop=False)
                        mm(acc[0:P, k * BANK:k * BANK + 2 * F], any_hTt[:, k, :], w2t[:], start=False,
                           stop=True).then_inc(any_g_ready, 1)
                pe.wait_ge(any_g_kept, nth(DTRIPS + 1, SLOTS - 1))
                aggregate(1)
                pe.wait_ge(any_wr_kept, 1)
                with pe.Fori(0, DTRIPS) as i:
                    for k in range(SLOTS):
                        pe.wait_ge(any_rows1_ready, nth(i + 1, k))
                        pe.wait_ge(any_y_kept, nth(i + 1, k))
                        nc.tensor.transpose(acc[:, k * BANK:k * BANK + P], g_row_x[:, k, :],
                                            ident[0:P, 0:P]).then_inc(any_turned1, 1)
                    for k in range(SLOTS):
                        pe.wait_ge(any_cols1_ready, nth(i + 1, k))
                        mm(acc[0:P, k * BANK:k * BANK + R * F], g_cols[:, k, 0, 0:P], g_wrT[:].rearrange("p r f -> p (r f)"),
                           start=True, stop=True).then_inc(any_y_ready, 1)
                pe.wait_ge(any_y_kept, nth(DTRIPS + 1, SLOTS - 1))
                aggregate(2)



_INS = ["x", "edges", "edge_weight", "L0_gnn_W_self1", "L0_gnn_W_neigh1", "L0_gnn_b1",
        "L0_gnn_W_self2", "L0_gnn_W_neigh2", "L0_gnn_b2", "L1_gnn_W", "L1_gnn_gamma", "L1_gnn_beta",
        "L1_gnn_running_mean", "L1_gnn_running_var"]


def kernel(**inputs):
    import numpy as np
    import concourse.bacc as bacc
    from concourse.bass_utils import run_bass_kernel_spmd

    nc = bacc.Bacc("TRN2", target_bir_lowering=False, num_devices=1)
    arrays, args = {}, []
    src, dst, etype = (inputs[n] for n in ("src", "dst", "edge_type_3"))
    inputs["edges"] = np.stack([src, dst, etype, np.append(dst[1:], np.array(-1, dst.dtype))])
    for name in _INS:
        a = np.ascontiguousarray(inputs[name])
        arrays[f"in_{name}"] = a
        args.append(nc.dram_tensor(f"in_{name}", a.shape, mybir.dt.from_np(a.dtype), kind="ExternalInput").ap())
    out = nc.dram_tensor("out", arrays["in_x"].shape, F32, kind="ExternalOutput").ap()
    gnn_block(nc, *args, out)
    r = run_bass_kernel_spmd(nc, [arrays], core_ids=[0])
    return r.results[0]["out"]
```
